# Optimizing a Trainium2 kernel written in Bass

```python
import numpy as np
import jax
import jax.numpy as jnp

def _softmax(x, axis=-1):
    return jax.nn.softmax(x, axis=axis)

def _gelu(x):
    return jax.nn.gelu(x, approximate=True)

def _silu(x):
    return jax.nn.silu(x)

def _sigmoid(x):
    return jax.nn.sigmoid(x)

def _layernorm(x, axis=-1, eps=1e-05):
    m = jnp.mean(x, axis=axis, keepdims=True)
    v = jnp.var(x, axis=axis, keepdims=True)
    return (x - m) / jnp.sqrt(v + eps)

def _scatter_add(tgt, idx, src, axis=0):
    return tgt.at[idx].add(src)

def _segment_sum(src, seg, n):
    return jax.ops.segment_sum(src, seg, n)
kernel_name = 'mk_seq_postln_d1_jaxref_r4_80ed1f'

def setup_inputs(seed: int=0):
    np.random.seed(seed)
    _w = jnp.asarray

    def _L0_attn_setup():
        import jax, jax.numpy as jnp
        import numpy as np
        N_HEADS = 16
        WINDOW = 128
        EPS = 1e-06
        NEG_INF = -1e+30

        def _l2norm(t):
            n = jnp.sqrt(jnp.sum(t * t, axis=-1, keepdims=True))
            return t / jnp.maximum(n, EPS)
        key = jax.random.key(seed)
        ks = jax.random.split(key, 5)
        B, T, D = (2, 512, 256)
        scale = 1.0 / np.sqrt(D)
        return {'x': jax.random.normal(ks[0], (B, T, D), dtype=jnp.float32), 'Wq': jax.random.normal(ks[1], (D, D), dtype=jnp.float32) * scale, 'Wk': jax.random.normal(ks[2], (D, D), dtype=jnp.float32) * scale, 'Wv': jax.random.normal(ks[3], (D, D), dtype=jnp.float32) * scale, 'Wo': jax.random.normal(ks[4], (D, D), dtype=jnp.float32) * scale}
    _L0_attn_in = _L0_attn_setup()

    def _L0_ffn_setup():
        import jax, jax.numpy as jnp
        import numpy as np

        def _binarize(w):
            alpha = jax.lax.stop_gradient(jnp.mean(jnp.abs(w), axis=1, keepdims=True))
            bw = alpha * jnp.sign(w)
            return w + jax.lax.stop_gradient(bw - w)
        key = jax.random.key(seed)
        k1, k2, k3, k4, k5 = jax.random.split(key, 5)
        D, H = (256, 1024)
        x = jax.random.normal(k1, (64, 196, D), dtype=jnp.float32)
        w1 = jax.random.normal(k2, (H, D), dtype=jnp.float32) * 0.02
        b1 = jax.random.normal(k3, (H,), dtype=jnp.float32) * 0.02
        w2 = jax.random.normal(k4, (D, H), dtype=jnp.float32) * 0.02
        b2 = jax.random.normal(k5, (D,), dtype=jnp.float32) * 0.02
        return {'x': x, 'w1': w1, 'b1': b1, 'w2': w2, 'b2': b2}
    _L0_ffn_in = _L0_ffn_setup()
    _d = {'L0_attn_x': _L0_attn_in['x'], 'L0_attn_Wq': _L0_attn_in['Wq'], 'L0_attn_Wk': _L0_attn_in['Wk'], 'L0_attn_Wv': _L0_attn_in['Wv'], 'L0_attn_Wo': _L0_attn_in['Wo'], 'L0_ffn_w1': _L0_ffn_in['w1'], 'L0_ffn_b1': _L0_ffn_in['b1'], 'L0_ffn_w2': _L0_ffn_in['w2'], 'L0_ffn_b2': _L0_ffn_in['b2']}
    _x0 = _d['L0_attn_x']
    _d['L0_attn_x'] = jax.random.normal(jax.random.fold_in(jax.random.key(seed), 1), (1, 4096, 256), dtype=_x0.dtype)
    del _x0
    return _d

def reference(L0_attn_x, L0_attn_Wq, L0_attn_Wk, L0_attn_Wv, L0_attn_Wo, L0_ffn_w1, L0_ffn_b1, L0_ffn_w2, L0_ffn_b2):

    def _L0_attn_ref(x, Wq, Wk, Wv, Wo):
        import jax, jax.numpy as jnp
        import numpy as np
        N_HEADS = 16
        WINDOW = 128
        EPS = 1e-06
        NEG_INF = -1e+30

        def _l2norm(t):
            n = jnp.sqrt(jnp.sum(t * t, axis=-1, keepdims=True))
            return t / jnp.maximum(n, EPS)
        B, T, D = x.shape
        H, hd = (N_HEADS, D // N_HEADS)

        def proj(W):
            return jnp.einsum('btd,ed->bte', x, W).reshape(B, T, H, hd).transpose(0, 2, 1, 3)
        q = _l2norm(proj(Wq))
        k = _l2norm(proj(Wk))
        v = proj(Wv)
        attn = jnp.einsum('bhqd,bhkd->bhqk', q, k)
        pos = jnp.arange(T)
        rel = pos[None, :] - pos[:, None]
        mask = (rel < 0) | (rel >= WINDOW)
        base = jnp.linspace(0.0, 1.0, H, dtype=x.dtype)
        slopes = jnp.power(jnp.asarray(2.0, x.dtype), -(8.0 * base))
        alibi = -jnp.abs(rel).astype(x.dtype)[None, :, :] * slopes[:, None, None]
        bias = jnp.where(mask[None, :, :], jnp.asarray(NEG_INF, x.dtype), alibi)
        attn = jax.nn.softmax(attn + bias[None], axis=-1)
        out = jnp.einsum('bhqk,bhkd->bhqd', attn, v)
        out = out.transpose(0, 2, 1, 3).reshape(B, T, D)
        return jnp.einsum('btd,ed->bte', out, Wo)

    def _L0_ffn_ref(x, w1, b1, w2, b2):
        import jax, jax.numpy as jnp
        import numpy as np

        def _binarize(w):
            alpha = jax.lax.stop_gradient(jnp.mean(jnp.abs(w), axis=1, keepdims=True))
            bw = alpha * jnp.sign(w)
            return w + jax.lax.stop_gradient(bw - w)
        bw1 = _binarize(w1)
        h = jnp.einsum('bsd,hd->bsh', x, bw1) + b1
        h = jax.nn.gelu(h, approximate=False)
        bw2 = _binarize(w2)
        out = jnp.einsum('bsh,dh->bsd', h, bw2) + b2
        return out
    x = L0_attn_x
    x = _layernorm(x + _L0_attn_ref(x, L0_attn_Wq, L0_attn_Wk, L0_attn_Wv, L0_attn_Wo), axis=-1)
    x = _layernorm(x + _L0_ffn_ref(x, L0_ffn_w1, L0_ffn_b1, L0_ffn_w2, L0_ffn_b2), axis=-1)
    return x

_drawn_inputs = setup_inputs


def setup_inputs(seed=0):
    import zlib

    import numpy as np

    out = dict(_drawn_inputs(seed))
    spreads = {}
    factors = {'L0_ffn_b1': 8.0, 'L0_ffn_b2': 2.923}
    for name, (base, spread) in spreads.items():
        noise = np.random.default_rng([zlib.crc32(name.encode()), seed]).standard_normal(out[name].shape)
        drawn = base * np.exp(spread * noise) if base else spread * noise
        out[name] = jnp.asarray(drawn.astype(out[name].dtype))
    for name, factor in factors.items():
        out[name] = (out[name] * factor).astype(out[name].dtype)
    return out
```

```python
from contextlib import ExitStack

import numpy as np

import concourse.bass as bass
from concourse import mybir

F32 = mybir.dt.float32
F16 = mybir.dt.float16
I32 = mybir.dt.int32
ALU = mybir.AluOpType
ACT = mybir.ActivationFunctionType
AX = mybir.AxisListType

P = 128
D = 256
DC = D // P
T = 4096
NB = T // P
H = 16
HD = D // H
PAIRS = H // 2
CH = 4
NC = H // CH
HID = 1024
HC = HID // P
GB = 4
NG = NB // GB
QK_SCALE = 2.0 ** 10
Y_SCALE = 2.0 ** 11
NORM_EPS = 1e-6
LN_EPS = 1e-5
FAR = 1.0e5
SLOPES = [2.0 ** (-8.0 * h / (H - 1)) for h in range(H)]
SEED_BASE = float(0x5F3759DF - (1 << 22) - (1 << 30))
NEWTON_OPS = 10


def count(sem_engine, sem, value):
    if isinstance(value, int) and value <= 0:
        return
    sem_engine.wait_ge(sem, value)


def build(nc, x, xT, wqkvT, woT, w1, w1T, b1c, w2T, b2, out):
    with ExitStack() as ctx:
        def sb(name, shape, dt=F32):
            return ctx.enter_context(nc.sbuf_tensor(name, shape, dt))

        def sem(name):
            return ctx.enter_context(nc.semaphore(name))

        wqkv = sb("wqkv", [P, DC, 3 * D])
        wo = sb("wo", [P, DC, D])
        w1_nat = sb("w1_nat", [P, HC, D])
        w1_t = sb("w1_t", [P, DC, HID])
        w2_t = sb("w2_t", [P, HC, D])
        sgn1 = sb("sgn1", [P, DC, HID], F16)
        sgn2 = sb("sgn2", [P, HC, D])
        bias1 = sb("bias1", [P, HC])
        bias2 = sb("bias2", [P, D])
        alpha1 = sb("alpha1", [P, HC])
        alpha2 = sb("alpha2", [P, D])
        mean_ones = sb("mean_ones", [P, P])
        id16 = sb("id16", [P, P], F16)
        id32 = sb("id32", [P, P])
        rel_i = sb("rel_i", [P, 3, P], I32)
        rel = sb("rel", [P, 3, P])
        alibi = sb("alibi", [P, H, 3 * P])
        xt = sb("xt", [P, 2, DC, P])
        resid = sb("resid", [P, NB, D])
        sq = sb("sq", [P, 2 * D])
        ss = sb("ss", [P, 2 * H])
        half = sb("half", [P, 2 * H])
        nt_a = sb("nt_a", [P, 2 * H])
        nt_b = sb("nt_b", [P, 2 * H])
        rnorm = sb("rnorm", [P, 2 * H])
        qkn = sb("qkn", [P, 2 * D])
        parts = sb("parts", [P, 2, 2 * H, 4, HD], F16)
        qT = sb("qT", [P, PAIRS, 2, P], F16)
        kTz = sb("kTz", [P, 2, PAIRS, P], F16)
        vsb = sb("vsb", [P, 2, H, HD + 1])
        prob = sb("prob", [P, 2, H, 2 * P])
        strips = sb("strips", [P, CH, P])
        rden = sb("rden", [P, H])
        otok = sb("otok", [P, D])
        oT = sb("oT", [P, DC, P])
        stats = sb("stats", [P, 6])
        mv_new = sb("mv_new", [P, 2])
        mv = sb("mv", [P, NB, 2])
        rstd = sb("rstd", [P, NB, 1])
        yparts = sb("yparts", [P, GB, 2, D], F16)
        yT = sb("yT", [P, 2, DC, GB, P], F16)
        hid = prob[:].rearrange("p s h c -> p s (h c)").rearrange("p s (k n) -> p s k n", k=HC)
        z = sb("z", [P, 2, GB, D])
        neg = sb("neg", [P, HC * D], F16)
        zstats = sb("zstats", [P, 6])
        zmv = sb("zmv", [P, GB, 2])
        zrstd = sb("zrstd", [P, GB])

        ps = ctx.enter_context(nc.psum_tensor("ps", [P, 8, 512], F32))
        QK, VO, TR, SC, OT = 0, 1, 2, 3, 7
        tr16 = ps[:, TR, :].bitcast(F16)
        YT, HB, ZB = 0, 2, 6
        yt16 = ps[:, YT:YT + 2, :].bitcast(F16)

        x_in = [sem("x_in_even"), sem("x_in_odd")]
        wqkv_in, wo_in, mlp_in = sem("wqkv_in"), sem("wo_in"), sem("mlp_in")
        consts = sem("consts")
        id_zero, rel_made, rel_cut, rel_f = sem("id_zero"), sem("rel_made"), sem("rel_cut"), sem("rel_f")
        alibi_done = sem("alibi_done")
        qkproj_done, sq_done, ss_done, newton, qkn_done = (
            sem(n) for n in ("qkproj_done", "sq_done", "ss_done", "newton", "qkn_done"))
        hi_ready, lo_ready, parts_ready = sem("hi_ready"), sem("lo_ready"), sem("parts_ready")
        tq_done, q_ready, tk_done, k_ready = (sem(n) for n in ("tq_done", "q_ready", "tk_done", "k_ready"))
        v_done, v_ready = sem("v_done"), sem("v_ready")
        s_done, exp_done, p_ready = sem("s_done"), sem("exp_done"), sem("p_ready")
        pv_done, strips_ready, otok_done = sem("pv_done"), sem("strips_ready"), sem("otok_done")
        rden_done, onorm_done = sem("rden_done"), sem("onorm_done")
        ot_done, ot_ready, wo_done = sem("ot_done"), sem("ot_ready"), sem("wo_done")
        resid_done, stats_done, aggr_done, mv_done = (
            sem(n) for n in ("resid_done", "stats_done", "aggr_done", "mv_done"))
        prep = sem("prep")
        sgn_step, sgn_ready = sem("sgn_step"), sem("sgn_ready")
        alpha2_done, abs_done = sem("alpha2_done"), sem("abs_done")
        y_done, yhi_done, ylo_done, yb_done = (sem(n) for n in ("y_done", "yhi_done", "ylo_done", "yb_done"))
        ty_done, yT_ready = sem("ty_done"), sem("yT_ready")
        h_done, gelu_done, ffn2_done = sem("h_done"), sem("gelu_done"), sem("ffn2_done")
        zscaled, zsum, zstat, zaggr = (sem(n) for n in ("zscaled", "zsum", "zstat", "zaggr"))
        znewton, z_ready = sem("znewton"), sem("z_ready")
        stored = [sem("stored_even"), sem("stored_odd")]

        block = ctx.enter_context(nc.Block())

        @block.sync
        def _(sp):
            def load_block(n, par):
                count(sp, v_done, n - 1)
                sp.dma_start(xt[:, par], xT[n]).then_inc(x_in[par], 16)
                sp.dma_start(resid[:, n, :], x[n]).then_inc(x_in[par], 16)

            sp.dma_start(wqkv[:], wqkvT).then_inc(wqkv_in, 16)
            load_block(0, 0)
            load_block(1, 1)
            sp.dma_start(wo[:], woT).then_inc(wo_in, 16)
            for dst, src in ((w1_t, w1T), (w2_t, w2T), (w1_nat, w1), (bias1, b1c), (bias2, b2)):
                sp.dma_start(dst[:], src).then_inc(mlp_in, 16)
            with sp.Fori(0, (NB - 2) // 2) as t:
                for par in range(2):
                    load_block(t * 2 + 2 + par, par)

            def store_group(g, par):
                sp.wait_ge(z_ready, g * GB + GB)
                sp.dma_start(out[g], z[:, par]).then_inc(stored[par], 16)

            with sp.Fori(0, NG // 2) as t:
                for par in range(2):
                    store_group(t * 2 + par, par)
            for par in range(2):
                sp.wait_ge(stored[par], 16 * NG // 2)

        @block.tensor
        def _(pe):
            def scores(i, c, par):
                pe.wait_ge(k_ready, i + 1)
                count(pe, exp_done, i * NC + c - 1)
                for j in range(CH):
                    h = CH * c + j
                    mm = nc.tensor.matmul(ps[:, SC + 2 * (c % 2) + j // 2, 256 * (j % 2):256 * (j % 2) + 256],
                                          kTz[:, h % 2, h // 2, :], qT[:, h // 2, :, :], start=True, stop=True)
                mm.then_inc(s_done, 1)

            def weighted_sum(i, c, par, cur):
                if c == 0:
                    pe.wait_ge(v_ready, i + 1 if cur else NB)
                    count(pe, strips_ready, i - 1)
                pe.wait_ge(p_ready, i * NC + c + 1 if cur else NB * NC)
                tiles = [1 - par, par] if cur else [1 - par]
                for n, s in enumerate(tiles):
                    for j in range(CH):
                        h = CH * c + j
                        mm = nc.tensor.matmul(ps[32 * j:32 * j + HD + 1, OT, P * c:P * c + P], vsb[:, s, h, :],
                                              prob[:, s, h, P * (1 - par):P * (1 - par) + P],
                                              start=(n == 0), stop=(n == len(tiles) - 1))
                if c == NC - 1:
                    mm.then_inc(pv_done, 1)

            def step(i, par, cur=True, pv=True, prev2=True, next1=True, next2=True):
                if cur:
                    scores(i, 0, par)
                    scores(i, 1, par)
                if prev2:
                    pe.wait_ge(strips_ready, i - 1)
                    pe.wait_ge(qkn_done, i + 2 if next1 else NB)
                    for c in range(NC):
                        mm = nc.tensor.transpose(ps[:, QK, P * c:P * c + P], strips[:, c, :], id32[:])
                    mm.then_inc(otok_done, 1)
                if cur:
                    scores(i, 2, par)
                if next2:
                    pe.wait_ge(x_in[par], (i + 2 - par) * 16 + 32)
                    count(pe, qkn_done, i + 2)
                    if prev2:
                        pe.wait_ge(onorm_done, i - 1)
                    for k in range(DC):
                        mm = nc.tensor.matmul(ps[:, QK, :], xt[:, par, k, :], wqkv[:, k, 0:2 * D],
                                              start=(k == 0), stop=(k == DC - 1))
                    mm.then_inc(qkproj_done, 1)
                if prev2:
                    pe.wait_ge(onorm_done, i - 1)
                    pe.wait_ge(v_ready, i + 1 if cur else NB)
                    for k in range(DC):
                        mm = nc.tensor.transpose(ps[:, VO, P * k:P * k + P], otok[:, P * k:P * k + P], id32[:])
                    mm.then_inc(ot_done, 1)
                if cur:
                    scores(i, 3, par)
                if pv:
                    weighted_sum(i, 0, par, cur)
                    weighted_sum(i, 1, par, cur)
                if prev2:
                    pe.wait_ge(ot_ready, i - 1)
                    for k in range(DC):
                        mm = nc.tensor.matmul(ps[:, VO, D:2 * D], oT[:, k, :], wo[:, k, :],
                                              start=(k == 0), stop=(k == DC - 1))
                    mm.then_inc(wo_done, 1)
                if next1:
                    pe.wait_ge(parts_ready, i + 2)
                    count(pe, k_ready, i + 1)
                    for m in range(PAIRS):
                        src = parts[:, 1 - par, 2 * m:2 * m + 2, :, :].rearrange("p h a d -> p (h a d)")
                        mm = nc.tensor.transpose(tr16[:, P * m:P * m + P], src, id16[:])
                    mm.then_inc(tq_done, 1)
                if pv:
                    weighted_sum(i, 2, par, cur)
                if next1:
                    pe.wait_ge(q_ready, i + 2)
                    for m in range(PAIRS):
                        src = parts[:, 1 - par, H + 2 * m:H + 2 * m + 2, :, :].rearrange("p h a d -> p (h a d)")
                        mm = nc.tensor.transpose(tr16[:, P * m:P * m + P], src, id16[:])
                    mm.then_inc(tk_done, 1)
                if pv:
                    weighted_sum(i, 3, par, cur)
                if next1:
                    if prev2:
                        pe.wait_ge(resid_done, i - 1)
                    count(pe, v_ready, i + 1)
                    for k in range(DC):
                        mm = nc.tensor.matmul(ps[:, VO, 0:D], xt[:, 1 - par, k, :], wqkv[:, k, 2 * D:3 * D],
                                              start=(k == 0), stop=(k == DC - 1))
                    mm.then_inc(v_done, 1)

            pe.wait_ge(wqkv_in, 16)
            pe.wait_ge(consts, 7)
            step(-2, 0, cur=False, pv=False, prev2=False, next1=False)
            step(-1, 1, cur=False, pv=False, prev2=False)
            step(0, 0, pv=False, prev2=False)
            step(1, 1, prev2=False)
            pe.wait_ge(wo_in, 16)
            with pe.Fori(0, (NB - 4) // 2) as t:
                for par in range(2):
                    step(t * 2 + 2 + par, par)
            step(NB - 2, 0, next2=False)
            step(NB - 1, 1, next1=False, next2=False)
            step(NB, 0, cur=False, next1=False, next2=False)
            step(NB + 1, 1, cur=False, pv=False, next1=False, next2=False)

            pe.wait_ge(prep, 1)
            for k in range(HC):
                mm = nc.tensor.matmul(ps[:, ZB, 0:D], mean_ones[:], w2_t[:, k, :], start=(k == 0), stop=(k == HC - 1))
            mm.then_inc(alpha2_done, 1)

            def turn_y(n):
                pe.wait_ge(ylo_done, n * GB + GB)
                count(pe, yT_ready, n)
                for a in range(2):
                    for k in range(DC):
                        for b in range(GB):
                            at = ((a * DC + k) * GB + b) * P
                            mm = nc.tensor.transpose(ps[:, YT + at // 1024, :].bitcast(F16)[:, at % 1024:at % 1024 + P],
                                                     yparts[:, b, a, P * k:P * k + P], id16[:])
                mm.then_inc(ty_done, 1)

            def hidden(n, k):
                if k == 0:
                    pe.wait_ge(yT_ready, n + 1)
                count(pe, gelu_done, n * HC + k - 3)
                for m, (a, c) in enumerate((a, c) for a in range(2) for c in range(DC)):
                    mm = nc.tensor.matmul(ps[:, HB + k % 4, :], sgn1[:, c, P * k:P * k + P], yT[:, a, c, :, :],
                                          start=(m == 0), stop=(m == 2 * DC - 1))
                mm.then_inc(h_done, 1)

            def second(g, b, par):
                if b == 0:
                    pe.wait_ge(gelu_done, g * HC + HC)
                count(pe, zscaled, g * GB + b - 1)
                for k in range(HC):
                    mm = nc.tensor.matmul(ps[:, ZB + b % 2, 0:D], hid[:, par, k, P * b:P * b + P], sgn2[:, k, :],
                                          start=(k == 0), stop=(k == HC - 1))
                mm.then_inc(ffn2_done, 1)

            def group_step(g, par, cur=True, nxt=True):
                if nxt:
                    turn_y(g + 1)
                for b in range(GB):
                    if cur:
                        second(g, b, par)
                    if nxt:
                        hidden(g + 1, 2 * b)
                        hidden(g + 1, 2 * b + 1)

            pe.wait_ge(sgn_ready, 2)
            pe.wait_ge(prep, 2)
            group_step(-1, 1, cur=False)
            group_step(0, 0)
            with pe.Fori(0, (NG - 2) // 2) as t:
                for k, par in enumerate((1, 0)):
                    group_step(t * 2 + 1 + k, par)
            group_step(NG - 1, 1, nxt=False)

        @block.scalar
        def _(act):
            def step(i, par, cur=True, pv=True, prev2=True, next1=True, next2=True):
                if prev2:
                    act.wait_ge(pv_done, i - 1)
                    count(act, otok_done, i - 2)
                    nc.scalar.activation(strips[:], ps[:, OT, :].rearrange("p (c t) -> p c t", c=NC),
                                         ACT.Copy).then_inc(strips_ready, 1)

                def exps(c):
                    act.wait_ge(s_done, i * NC + c + 1)
                    if c == 0:
                        count(act, pv_done, i - 1)
                    nc.scalar.activation(prob[:, par, CH * c:CH * c + CH, :],
                                         ps[:, SC + 2 * (c % 2):SC + 2 * (c % 2) + 2, :],
                                         ACT.Exp, scale=QK_SCALE ** -2).then_inc(exp_done, 1)

                if cur:
                    exps(0)
                    exps(1)
                    exps(2)
                if next2:
                    act.wait_ge(qkproj_done, i + 3)
                    count(act, ss_done, i + 2)
                    nc.scalar.activation(sq[:], ps[:, QK, :], ACT.Square, scale=1 / QK_SCALE).then_inc(sq_done, 1)
                if prev2:
                    act.wait_ge(ot_done, i - 1)
                    count(act, wo_done, i - 2)
                    nc.scalar.activation(oT[:], ps[:, VO, 0:D].rearrange("p (k t) -> p k t", k=DC),
                                         ACT.Copy).then_inc(ot_ready, 1)
                if cur:
                    exps(3)
                if next1:
                    act.wait_ge(tq_done, i + 2)
                    count(act, s_done, (i + 1) * NC)
                    nc.scalar.activation(qT[:, :, 1 - par, :], tr16.rearrange("p (m t) -> p m t", m=PAIRS),
                                         ACT.Copy).then_inc(q_ready, 1)
                if next2:
                    act.wait_ge(qkn_done, i + 3)
                    count(act, tk_done, i + 1)
                    src = qkn[:].rearrange("p (h d) -> p h d", d=HD)
                    nc.scalar.activation(parts[:, par, 0:H, 0, :], src[:, 0:H, :], ACT.Copy)
                    nc.scalar.activation(parts[:, par, H:2 * H, 0:2, :],
                                         src[:, H:2 * H, :].unsqueeze(2).to_broadcast([P, H, 2, HD]),
                                         ACT.Copy).then_inc(hi_ready, 1)
                if next1:
                    act.wait_ge(tk_done, i + 2)
                    for s in range(2):
                        rows = slice(64 * s, 64 * s + 64)
                        cp = nc.scalar.activation(kTz[rows, s, :, :],
                                                  tr16[rows, :].rearrange("p (m t) -> p m t", m=PAIRS), ACT.Copy)
                    cp.then_inc(k_ready, 1)
                    act.wait_ge(v_done, i + 2)
                    if pv:
                        act.wait_ge(pv_done, i)
                    nc.scalar.activation(vsb[:, 1 - par, :, 0:HD],
                                         ps[:, VO, 0:D].rearrange("p (h d) -> p h d", d=HD),
                                         ACT.Copy).then_inc(v_ready, 1)

            act.wait_ge(rel_f, 1)
            for h in range(H):
                fac = nc.scalar.activation(alibi[:, h, :], rel[:].rearrange("p a b -> p (a b)"), ACT.Exp,
                                           scale=-SLOPES[h])
            fac.then_inc(alibi_done, 1)
            act.wait_ge(consts, 7)
            step(-2, 0, cur=False, pv=False, prev2=False, next1=False)
            step(-1, 1, cur=False, pv=False, prev2=False)
            step(0, 0, pv=False, prev2=False)
            step(1, 1, prev2=False)
            with act.Fori(0, (NB - 4) // 2) as t:
                for par in range(2):
                    step(t * 2 + 2 + par, par)
            step(NB - 2, 0, next2=False)
            step(NB - 1, 1, next1=False, next2=False)
            step(NB, 0, cur=False, next1=False, next2=False)
            step(NB + 1, 1, cur=False, pv=False, next1=False, next2=False)

            def group_step(n, par):
                act.wait_ge(ty_done, n + 1)
                count(act, h_done, n * HC)
                for a in range(2):
                    cp = nc.scalar.activation(yT[:, a, :, :, :].rearrange("p c b t -> p (c b t)"),
                                              ps[:, YT + a, :].bitcast(F16), ACT.Copy)
                cp.then_inc(yT_ready, 1)
                count(act, ffn2_done, n * GB - GB)
                for k in range(HC):
                    act.wait_ge(h_done, n * HC + k + 1)
                    nc.scalar.activation(hid[:, par, k, :], ps[:, HB + k % 4, :], ACT.Gelu,
                                         bias=bias1[:, k:k + 1], scale=alpha1[:, k:k + 1]).then_inc(gelu_done, 1)

            act.wait_ge(prep, 3)
            act.wait_ge(mlp_in, 16 * 5)
            group_step(0, 0)
            group_step(1, 1)
            with act.Fori(0, (NG - 2) // 2) as t:
                for par in range(2):
                    group_step(t * 2 + 2 + par, par)

        @block.vector
        def _(dve):
            def rsqrt(s, half_, a, b, y, eps, op, done, base):
                nc.vector.tensor_scalar(half_, s, eps, -0.5, op, ALU.mult).then_inc(done, 1)
                dve.wait_ge(done, base + 1)
                nc.vector.tensor_scalar(y.bitcast(I32), half_.bitcast(I32), -0.5, SEED_BASE,
                                        ALU.mult, ALU.add).then_inc(done, 1)
                for r in range(3):
                    dve.wait_ge(done, base + 3 * r + 2)
                    nc.vector.tensor_tensor(a, half_, y, ALU.mult).then_inc(done, 1)
                    dve.wait_ge(done, base + 3 * r + 3)
                    nc.vector.tensor_tensor(b, a, y, ALU.mult).then_inc(done, 1)
                    dve.wait_ge(done, base + 3 * r + 4)
                    nc.vector.scalar_tensor_tensor(out=y, in0=b, scalar=1.5, in1=y, op0=ALU.add,
                                                   op1=ALU.mult).then_inc(done, 1)
                dve.wait_ge(done, base + NEWTON_OPS + 1)

            def step(i, par, cur=True, pv=True, prev2=True, next1=True, next2=True):
                def mask(c):
                    dve.wait_ge(exp_done, i * NC + c + 1)
                    tile = prob[:, par, CH * c:CH * c + CH, :]
                    nc.vector.tensor_tensor(tile, tile, alibi[:, CH * c:CH * c + CH, P * par:P * par + 2 * P],
                                            ALU.mult).then_inc(p_ready, 1)

                if next1:
                    dve.wait_ge(lo_ready, i + 2)
                    nc.vector.tensor_copy(parts[:, 1 - par, 0:H, 2:4, :],
                                          parts[:, 1 - par, 0:H, 0:2, :]).then_inc(parts_ready, 1)
                if cur:
                    mask(0)
                if prev2:
                    sums = ps[:, QK, :].rearrange("p (h d) -> p h d", d=32)
                    dve.wait_ge(otok_done, i - 1)
                    count(dve, onorm_done, i - 2)
                    nc.vector.reciprocal(rden[:], sums[:, :, HD]).then_inc(rden_done, 1)
                    dve.wait_ge(rden_done, i - 1)
                    count(dve, ot_done, i - 2)
                    nc.vector.tensor_tensor(otok[:].rearrange("p (h d) -> p h d", d=HD), sums[:, :, 0:HD],
                                            rden[:].unsqueeze(2).to_broadcast([P, H, HD]),
                                            ALU.mult).then_inc(onorm_done, 1)
                if cur:
                    mask(1)
                    mask(2)
                if next2:
                    dve.wait_ge(sq_done, i + 3)
                    nc.vector.tensor_reduce(ss[:], sq[:].rearrange("p (h d) -> p h d", d=HD), AX.X,
                                            ALU.add).then_inc(ss_done, 1)
                    dve.wait_ge(ss_done, i + 3)
                    count(dve, qkn_done, i + 2)
                    rsqrt(ss[:], half[:], nt_a[:], nt_b[:], rnorm[:], (NORM_EPS / QK_SCALE) ** 2, ALU.max,
                          newton, (i + 2) * (NEWTON_OPS + 1))
                    count(dve, lo_ready, i + 2)
                    nc.vector.tensor_tensor(qkn[:].rearrange("p (h d) -> p h d", d=HD),
                                            ps[:, QK, :].rearrange("p (h d) -> p h d", d=HD),
                                            rnorm[:].unsqueeze(2).to_broadcast([P, 2 * H, HD]),
                                            ALU.mult).then_inc(qkn_done, 1)
                if cur:
                    mask(3)
                if prev2:
                    dve.wait_ge(wo_done, i - 1)
                    dve.wait_ge(x_in[par], (i - 2 - par) * 16 + 32)
                    nc.vector.tensor_tensor(resid[:, i - 2, :], resid[:, i - 2, :], ps[:, VO, D:2 * D],
                                            ALU.add).then_inc(resid_done, 1)
                    dve.wait_ge(rel_cut, 3)
                    dve.wait_ge(resid_done, i - 1)
                    count(dve, aggr_done, i - 2)
                    nc.vector.bn_stats(stats[:], resid[:, i - 2, :]).then_inc(stats_done, 1)
                    dve.wait_ge(rel_cut, 3)
                    dve.wait_ge(stats_done, i - 1)
                    count(dve, mv_done, i - 2)
                    nc.vector.bn_aggr(mv_new[:], stats[:]).then_inc(aggr_done, 1)
                    dve.wait_ge(aggr_done, i - 1)
                    nc.vector.tensor_copy(mv[:, i - 2, :], mv_new[:]).then_inc(mv_done, 1)

            dve.wait_ge(rel_cut, 3)
            nc.vector.tensor_copy(rel[:], rel_i[:]).then_inc(rel_f, 1)
            nc.vector.memset(vsb[:], 1.0).then_inc(consts, 1)
            nc.vector.memset(ps[:, OT, :], 0.0).then_inc(consts, 1)
            nc.vector.memset(mean_ones[:], 1.0 / HID).then_inc(consts, 1)
            dve.wait_ge(alibi_done, 1)
            step(-2, 0, cur=False, pv=False, prev2=False, next1=False)
            step(-1, 1, cur=False, pv=False, prev2=False)
            step(0, 0, pv=False, prev2=False)
            step(1, 1, prev2=False)
            with dve.Fori(0, (NB - 4) // 2) as t:
                for par in range(2):
                    step(t * 2 + 2 + par, par)
            step(NB - 2, 0, next2=False)
            step(NB - 1, 1, next1=False, next2=False)

            dve.wait_ge(mlp_in, 16 * 5)
            dve.wait_ge(sgn_ready, 2)
            nc.vector.tensor_tensor(w2_t[:], w2_t[:], sgn2[:], ALU.mult).then_inc(prep, 1)
            step(NB, 0, cur=False, next1=False, next2=False)
            step(NB + 1, 1, cur=False, pv=False, next1=False, next2=False)
            dve.wait_ge(alpha2_done, 1)
            nc.vector.tensor_copy(alpha2[:], ps[:, ZB, 0:D]).then_inc(prep, 1)
            nc.vector.tensor_reduce(alpha1[:], w1_nat[:], AX.X, ALU.add, apply_absolute_value=True).then_inc(abs_done, 1)
            dve.wait_ge(abs_done, 1)
            nc.vector.tensor_scalar(alpha1[:], alpha1[:], 1.0 / (D * Y_SCALE), None, ALU.mult).then_inc(prep, 1)
            dve.wait_ge(mv_done, NB)
            done = NB * (NEWTON_OPS + 1)
            rsqrt(mv[:, :, 1], half[:], nt_a[:], nt_b[:], rstd[:, :, 0], LN_EPS, ALU.add, newton, done)

            def split_group(n):
                for b in range(GB):
                    m = n * GB + b
                    nc.vector.tensor_scalar(resid[:, m, :], resid[:, m, :], mv[:, m, 0:1], rstd[:, m, :],
                                            ALU.subtract, ALU.mult).then_inc(y_done, 1)
                    dve.wait_ge(y_done, m + 1)
                    if b == 0:
                        count(dve, ty_done, n)
                    nc.vector.tensor_scalar(yparts[:, b, 0, :], resid[:, m, :], Y_SCALE, None,
                                            ALU.mult).then_inc(yhi_done, 1)
                    dve.wait_ge(yhi_done, m + 1)
                    nc.vector.scalar_tensor_tensor(out=yparts[:, b, 1, :], in0=resid[:, m, :], scalar=Y_SCALE,
                                                   in1=yparts[:, b, 0, :], op0=ALU.mult,
                                                   op1=ALU.subtract).then_inc(ylo_done, 1)

            def finish_group(g, par):
                for b in range(GB):
                    m = g * GB + b
                    dve.wait_ge(ffn2_done, m + 1)
                    if b == 0:
                        count(dve, stored[par], (g - par) * 8)
                    nc.vector.tensor_tensor(z[:, par, b, :], ps[:, ZB + b % 2, 0:D], alpha2[:],
                                            ALU.mult).then_inc(zscaled, 1)
                    dve.wait_ge(zscaled, m + 1)
                    if b == 0:
                        dve.wait_ge(yb_done, g * GB + GB)
                    nc.vector.tensor_tensor(z[:, par, b, :], z[:, par, b, :], resid[:, m, :],
                                            ALU.add).then_inc(zsum, 1)
                    dve.wait_ge(zsum, m + 1)
                    count(dve, zaggr, m)
                    nc.vector.bn_stats(zstats[:], z[:, par, b, :]).then_inc(zstat, 1)
                    dve.wait_ge(rel_cut, 3)
                    dve.wait_ge(zstat, m + 1)
                    if b == 0:
                        count(dve, z_ready, g * GB)
                    nc.vector.bn_aggr(zmv[:, b, :], zstats[:]).then_inc(zaggr, 1)
                dve.wait_ge(zaggr, g * GB + GB)
                rsqrt(zmv[:, :, 1], half[:, 0:GB], nt_a[:, 0:GB], nt_b[:, 0:GB], zrstd[:], LN_EPS, ALU.add,
                      znewton, g * (NEWTON_OPS + 1))
                for b in range(GB):
                    nc.vector.tensor_scalar(z[:, par, b, :], z[:, par, b, :], zmv[:, b, 0:1], zrstd[:, b:b + 1],
                                            ALU.subtract, ALU.mult).then_inc(z_ready, 1)

            split_group(0)
            split_group(1)
            for par in range(2):
                split_group(2 + par)
                finish_group(par, par)
            with dve.Fori(0, (NG - 4) // 2) as t:
                for par in range(2):
                    split_group(t * 2 + 4 + par)
                    finish_group(t * 2 + 2 + par, par)
            finish_group(NG - 2, 0)
            finish_group(NG - 1, 1)

        @block.gpsimd
        def _(pool):
            for a in range(3):
                nc.gpsimd.iota(rel_i[:, a, :], pattern=[[-1, P]], base=P * (a % 2),
                               channel_multiplier=1).then_inc(rel_made, 1)
            nc.gpsimd.memset(id16[:], 0.0).then_inc(id_zero, 1)
            nc.gpsimd.memset(id32[:], 0.0).then_inc(id_zero, 1)
            pool.wait_ge(rel_made, 3)
            for a in range(3):
                near = a % 2
                nc.gpsimd.affine_select(out=rel_i[:, a, :], in_=rel_i[:, a, :], compare_op=ALU.is_ge, fill=FAR,
                                        base=-near, pattern=[[1 if near else -1, P]],
                                        channel_multiplier=-1 if near else 1).then_inc(rel_cut, 1)
            pool.wait_ge(id_zero, 2)
            for m in (id16, id32):
                nc.gpsimd.affine_select(out=m[:], in_=m[:], compare_op=ALU.not_equal, fill=1.0, base=0,
                                        pattern=[[-1, P]], channel_multiplier=1).then_inc(consts, 1)
            nc.gpsimd.memset(qT[:], 0.0).then_inc(consts, 1)
            nc.gpsimd.memset(kTz[:], 0.0).then_inc(consts, 1)

            def low_part(n, par):
                pool.wait_ge(hi_ready, n + 1)
                src = qkn[:].rearrange("p (h d) -> p h d", d=HD)
                nc.gpsimd.tensor_tensor(parts[:, par, 0:H, 1, :], src[:, 0:H, :], parts[:, par, 0:H, 0, :],
                                        ALU.subtract)
                nc.gpsimd.tensor_tensor(parts[:, par, H:2 * H, 2:4, :],
                                        src[:, H:2 * H, :].unsqueeze(2).to_broadcast([P, H, 2, HD]),
                                        parts[:, par, H:2 * H, 0:2, :], ALU.subtract).then_inc(lo_ready, 1)

            with pool.Fori(0, NB // 2) as t:
                for par in range(2):
                    low_part(t * 2 + par, par)

            pool.wait_ge(mlp_in, 16 * 5)
            for n, (w, s) in enumerate(((w1_t, sgn1), (w2_t, sgn2))):
                count(pool, sgn_ready, n)
                below = neg[:].rearrange("p (a b) -> p a b", a=w.shape[1])
                nc.gpsimd.tensor_scalar(s[:], w[:], 0.0, None, ALU.is_gt).then_inc(sgn_step, 1)
                nc.gpsimd.tensor_scalar(below, w[:], 0.0, None, ALU.is_lt).then_inc(sgn_step, 1)
                pool.wait_ge(sgn_step, 2 * n + 2)
                nc.gpsimd.tensor_tensor(s[:], s[:], below, ALU.subtract).then_inc(sgn_ready, 1)

            def add_b2(m):
                pool.wait_ge(ylo_done, m + 1)
                nc.gpsimd.tensor_tensor(resid[:, m, :], resid[:, m, :], bias2[:], ALU.add).then_inc(yb_done, 1)

            with pool.Fori(0, NB) as m:
                add_b2(m)


_OUT = "out_dram"


def kernel(L0_attn_x, L0_attn_Wq, L0_attn_Wk, L0_attn_Wv, L0_attn_Wo, L0_ffn_w1, L0_ffn_b1, L0_ffn_w2, L0_ffn_b2):
    import concourse.bacc as bacc
    from concourse.bass_utils import run_bass_kernel_spmd

    def cont(a):
        return np.ascontiguousarray(a)

    x = np.asarray(L0_attn_x).reshape(NB, P, D)
    wqkv = np.concatenate([np.asarray(w) for w in (L0_attn_Wq, L0_attn_Wk, L0_attn_Wv)], axis=0)
    arrays = {
        "x": cont(x),
        "xT": cont(x.reshape(NB, P, DC, P).transpose(0, 3, 2, 1)),
        "wqkvT": cont(wqkv.T.reshape(DC, P, 3 * D).transpose(1, 0, 2)),
        "woT": cont(np.asarray(L0_attn_Wo).T.reshape(DC, P, D).transpose(1, 0, 2)),
        "w1": cont(np.asarray(L0_ffn_w1).reshape(HC, P, D).transpose(1, 0, 2)),
        "w1T": cont(np.asarray(L0_ffn_w1).T.reshape(DC, P, HID).transpose(1, 0, 2)),
        "b1c": cont(np.asarray(L0_ffn_b1).reshape(HC, P).T),
        "w2T": cont(np.asarray(L0_ffn_w2).T.reshape(HC, P, D).transpose(1, 0, 2)),
        "b2": cont(np.broadcast_to(np.asarray(L0_ffn_b2), (P, D))),
    }
    nc = bacc.Bacc("TRN2", target_bir_lowering=False, num_devices=1)
    args = [nc.dram_tensor(f"in_{n}", a.shape, F32, kind="ExternalInput").ap() for n, a in arrays.items()]
    out = nc.dram_tensor(_OUT, (T, D), F32, kind="ExternalOutput").ap()
    build(nc, *args, out.rearrange("(g b p) d -> g p b d", b=GB, p=P))
    r = run_bass_kernel_spmd(nc, [{f"in_{n}": a for n, a in arrays.items()}], core_ids=[0])
    return r.results[0][_OUT].reshape(1, T, D)
```

```python
from contextlib import ExitStack

import numpy as np

import concourse.bass as bass
from concourse import mybir

F32 = mybir.dt.float32
F16 = mybir.dt.float16
I32 = mybir.dt.int32
ALU = mybir.AluOpType
ACT = mybir.ActivationFunctionType
AX = mybir.AxisListType

P = 128
D = 256
DC = D // P
T = 4096
NB = T // P
H = 16
HD = D // H
XS = 4
PAIRS = H // 2
CH = 4
NC = H // CH
HID = 1024
HC = HID // P
GB = 4
NG = NB // GB
QK_SCALE = 2.0 ** 10
Y_SCALE = 2.0 ** 11
NORM_EPS = 1e-6
LN_EPS = 1e-5
TH = CH
EARLY = NB - 2 * GB
FAR = 1.0e5
SLOPES = [2.0 ** (-8.0 * h / (H - 1)) for h in range(H)]
SEED_BASE = float(0x5F3759DF - (1 << 22) - (1 << 30))
NEWTON_OPS = 10


def count(sem_engine, sem, value):
    if isinstance(value, int) and value <= 0:
        return
    sem_engine.wait_ge(sem, value)


def build(nc, x, xT, wqkvT, woT, w1, w1T, b1c, w2T, b2, out):
    with ExitStack() as ctx:
        def sb(name, shape, dt=F32):
            return ctx.enter_context(nc.sbuf_tensor(name, shape, dt))

        def sem(name):
            return ctx.enter_context(nc.semaphore(name))

        wqkv = sb("wqkv", [P, DC, 3 * D])
        wo = sb("wo", [P, DC, D])
        w1_nat = sb("w1_nat", [P, HC, D])
        w1_t = sb("w1_t", [P, DC, HID])
        w2_t = sb("w2_t", [P, HC, D])
        sgn1 = sb("sgn1", [P, DC, HID], F16)
        sgn2 = sb("sgn2", [P, HC, D], F16)
        bias1 = sb("bias1", [P, HC])
        bias2 = sb("bias2", [P, D])
        alpha1 = sb("alpha1", [P, HC])
        alpha2 = sb("alpha2", [P, D])
        mean_ones = sb("mean_ones", [P, P])
        id16 = sb("id16", [P, P], F16)
        id32 = sb("id32", [P, P])
        rel_i = sb("rel_i", [P, 3, P], I32)
        rel = sb("rel", [P, 3, P])
        alibi = sb("alibi", [P, TH, 3 * P])
        far_key = sb("far_key", [P, 1])
        fade = sb("fade", [P, 2, H - TH, HD + 1])
        xt = sb("xt", [P, XS, DC, P])
        resid = sb("resid", [P, NB, D])
        sq = sb("sq", [P, 2 * D])
        ss = sb("ss", [P, 2 * H])
        half = sb("half", [P, 2 * H])
        nt_a = sb("nt_a", [P, 2 * H])
        nt_b = sb("nt_b", [P, 2 * H])
        rnorm = sb("rnorm", [P, 2 * H])
        qkn = sb("qkn", [P, 2 * D])
        parts = sb("parts", [P, 2, 2 * H, 4, HD], F16)
        qT = sb("qT", [P, PAIRS, 2, P], F16)
        kTz = sb("kTz", [P, 2, PAIRS, P], F16)
        vsb = sb("vsb", [P, 2, H, HD + 1])
        vdiag = sb("vdiag", [P, 2, H - TH, HD + 1])
        vnext = sb("vnext", [P, H - TH, HD + 1])
        prob = sb("prob", [P, 2, H, 2 * P])
        strips = sb("strips", [P, CH, P])
        rden = sb("rden", [P, H])
        otok = sb("otok", [P, D])
        oT = sb("oT", [P, DC, P])
        stats = sb("stats", [P, 6])
        mv_new = sb("mv_new", [P, 2])
        mv = sb("mv", [P, NB, 2])
        rstd = sb("rstd", [P, NB, 1])
        yparts = sb("yparts", [P, GB, 2, D], F16)
        yT = sb("yT", [P, 2, DC, GB, P], F16)
        gelu = sb("gelu", [P, 4, GB * P])
        hid = prob[:].rearrange("p s h c -> p s (h c)").bitcast(F16).rearrange("p s (a k n) -> p s a k n", a=2, k=HC)
        bound = sb("bound", [P, HC])
        hpos = sb("hpos", [P, HC])
        bound1 = sb("bound1", [P, 1])
        h_scale = sb("h_scale", [P, 1])
        h_unscale = sb("h_unscale", [P, 1])
        z = sb("z", [P, 2, GB, D])
        zstats = sb("zstats", [P, 6])
        zmv = sb("zmv", [P, GB, 2])
        zrstd = sb("zrstd", [P, GB])

        ps = ctx.enter_context(nc.psum_tensor("ps", [P, 8, 512], F32))
        QK, VO, TR, SC, OT = 0, 1, 2, 3, 7
        tr16 = ps[:, TR, :].bitcast(F16)
        YT, ZB, A2 = 3, 0, 6
        HB = (5, 6, 2, 7)

        x_in = [sem(f"x_in_{n}") for n in range(XS)]
        wqkv_in, wo_in, mlp_in = sem("wqkv_in"), sem("wo_in"), sem("mlp_in")
        consts = sem("consts")
        id_zero, rel_made, rel_cut, rel_f = sem("id_zero"), sem("rel_made"), sem("rel_cut"), sem("rel_f")
        alibi_done = sem("alibi_done")
        qkproj_done, sq_done, ss_done, newton, qkn_done = (
            sem(n) for n in ("qkproj_done", "sq_done", "ss_done", "newton", "qkn_done"))
        hi_ready, lo_ready, parts_ready = sem("hi_ready"), sem("lo_ready"), sem("parts_ready")
        tq_done, q_ready, tk_done, k_ready = (sem(n) for n in ("tq_done", "q_ready", "tk_done", "k_ready"))
        v_done, v_ready, vdiag_ready, vfade_ready = (sem(n) for n in ("v_done", "v_ready", "vdiag_ready", "vfade_ready"))
        s_done, exp_done = sem("s_done"), sem("exp_done")
        table_ready, cut_ready = sem("table_ready"), sem("cut_ready")
        pv_done, strips_ready, otok_done = sem("pv_done"), sem("strips_ready"), sem("otok_done")
        rden_done, onorm_done = sem("rden_done"), sem("onorm_done")
        ot_done, ot_ready, wo_done = sem("ot_done"), sem("ot_ready"), sem("wo_done")
        resid_done, stats_done, aggr_done, mv_done = (
            sem(n) for n in ("resid_done", "stats_done", "aggr_done", "mv_done"))
        prep = sem("prep")
        sgn_ready = sem("sgn_ready")
        alpha2_done, abs_done = sem("alpha2_done"), sem("abs_done")
        bound_done, bound_all = sem("bound_done"), sem("bound_all")
        y_done, yhi_done, ylo_done, yb_done = (sem(n) for n in ("y_done", "yhi_done", "ylo_done", "yb_done"))
        ty_done, yT_ready = sem("ty_done"), sem("yT_ready")
        h_done, gelu_done, hhi_done, hlo_done = (sem(n) for n in ("h_done", "gelu_done", "hhi_done", "hlo_done"))
        ffn2_done = sem("ffn2_done")
        zscaled, zsum, zstat, zaggr = (sem(n) for n in ("zscaled", "zsum", "zstat", "zaggr"))
        znewton, z_ready = sem("znewton"), sem("z_ready")
        stored = [sem("stored_even"), sem("stored_odd")]

        block = ctx.enter_context(nc.Block())

        @block.sync
        def _(sp):
            def load_block(n, slot):
                count(sp, v_done, n - XS + 1)
                sp.dma_start(xt[:, slot], xT[n]).then_inc(x_in[slot], 16)
                sp.dma_start(resid[:, n, :], x[n]).then_inc(x_in[slot], 16)

            sp.dma_start(wqkv[:, :, 0:2 * D], wqkvT[:, :, 0:2 * D]).then_inc(wqkv_in, 16)
            for n in range(XS):
                load_block(n, n)
            sp.dma_start(wqkv[:, :, 2 * D:3 * D], wqkvT[:, :, 2 * D:3 * D]).then_inc(wqkv_in, 16)
            sp.dma_start(wo[:], woT).then_inc(wo_in, 16)
            for dst, src in ((w1_t, w1T), (w2_t, w2T), (w1_nat, w1), (bias1, b1c), (bias2, b2)):
                sp.dma_start(dst[:], src).then_inc(mlp_in, 16)
            with sp.Fori(0, NB // XS - 1) as t:
                for slot in range(XS):
                    load_block(t * XS + XS + slot, slot)

            def store_group(g, par):
                sp.wait_ge(z_ready, g * GB + GB)
                sp.dma_start(out[g], z[:, par]).then_inc(stored[par], 16)

            with sp.Fori(0, NG // 2) as t:
                for par in range(2):
                    store_group(t * 2 + par, par)
            for par in range(2):
                sp.wait_ge(stored[par], 16 * NG // 2)

        @block.tensor
        def _(pe):
            def scores(i, c, par):
                pe.wait_ge(k_ready, i + 1)
                count(pe, exp_done, i * NC + c - 1)
                for j in range(CH):
                    h = CH * c + j
                    mm = nc.tensor.matmul(ps[:, SC + 2 * (c % 2) + j // 2, 256 * (j % 2):256 * (j % 2) + 256],
                                          kTz[:, h % 2, h // 2, :], qT[:, h // 2, :, :], start=True, stop=True)
                mm.then_inc(s_done, 1)

            def weighted_sum(i, c, par, cur):
                if c == 0:
                    pe.wait_ge(v_ready, i + 1 if cur else NB)
                    pe.wait_ge(table_ready, i + 1 if cur else NB)
                    count(pe, onorm_done, i - 1)
                elif c == 1:
                    pe.wait_ge(vfade_ready, i + 1 if cur else NB)
                if c > 0:
                    pe.wait_ge(cut_ready, i * (NC - 1) + c if cur else NB * (NC - 1))
                tiles = [1 - par, par] if cur else [1 - par]
                for n, s in enumerate(tiles):
                    for j in range(CH):
                        h = CH * c + j
                        if c == 0:
                            v = vsb[:, s, h, :]
                        else:
                            v = vdiag[:, s, h - TH, :] if n == 0 else vnext[:, h - TH, :]
                        mm = nc.tensor.matmul(ps[32 * j:32 * j + HD + 1, OT, P * c:P * c + P], v,
                                              prob[:, s, h, P * (1 - par):P * (1 - par) + P],
                                              start=(n == 0), stop=(n == len(tiles) - 1))
                if c == NC - 1:
                    mm.then_inc(pv_done, 1)

            def step(i, par, cur=True, pv=True, prev2=True, next1=True, next2=True, slot2=None, between=None):
                if slot2 is None:
                    slot2 = (i + 2) % XS
                if cur:
                    scores(i, 0, par)
                    scores(i, 1, par)
                if next2:
                    pe.wait_ge(x_in[slot2], (i + 2 - slot2) * (32 // XS) + 32)
                    count(pe, qkn_done, i + 2)
                    for k in range(DC):
                        mm = nc.tensor.matmul(ps[:, QK, :], xt[:, slot2, k, :], wqkv[:, k, 0:2 * D],
                                              start=(k == 0), stop=(k == DC - 1))
                    mm.then_inc(qkproj_done, 1)
                if prev2:
                    pe.wait_ge(strips_ready, i - 1)
                    for c in range(NC):
                        mm = nc.tensor.transpose(ps[:, OT, P * c:P * c + P], strips[:, c, :], id32[:])
                    mm.then_inc(otok_done, 1)
                if between:
                    between()
                if cur:
                    scores(i, 2, par)
                    scores(i, 3, par)
                if prev2:
                    pe.wait_ge(onorm_done, i - 1)
                    pe.wait_ge(v_ready, i + 1 if cur else NB)
                    for k in range(DC):
                        mm = nc.tensor.transpose(ps[:, VO, P * k:P * k + P], otok[:, P * k:P * k + P], id32[:])
                    mm.then_inc(ot_done, 1)
                if next1:
                    pe.wait_ge(parts_ready, i + 2)
                    count(pe, k_ready, i + 1)
                    for m in range(PAIRS):
                        src = parts[:, 1 - par, 2 * m:2 * m + 2, :, :].rearrange("p h a d -> p (h a d)")
                        mm = nc.tensor.transpose(tr16[:, P * m:P * m + P], src, id16[:])
                    mm.then_inc(tq_done, 1)
                if prev2:
                    pe.wait_ge(ot_ready, i - 1)
                    for k in range(DC):
                        mm = nc.tensor.matmul(ps[:, VO, D:2 * D], oT[:, k, :], wo[:, k, :],
                                              start=(k == 0), stop=(k == DC - 1))
                    mm.then_inc(wo_done, 1)
                if pv:
                    weighted_sum(i, 0, par, cur)
                    weighted_sum(i, 1, par, cur)
                if next1:
                    pe.wait_ge(q_ready, i + 2)
                    for m in range(PAIRS):
                        src = parts[:, 1 - par, H + 2 * m:H + 2 * m + 2, :, :].rearrange("p h a d -> p (h a d)")
                        mm = nc.tensor.transpose(tr16[:, P * m:P * m + P], src, id16[:])
                    mm.then_inc(tk_done, 1)
                    if prev2:
                        pe.wait_ge(resid_done, i - 1)
                    count(pe, v_ready, i + 1)
                    for k in range(DC):
                        mm = nc.tensor.matmul(ps[:, VO, 0:D], xt[:, (slot2 - 1) % XS, k, :], wqkv[:, k, 2 * D:3 * D],
                                              start=(k == 0), stop=(k == DC - 1))
                    mm.then_inc(v_done, 1)
                if pv:
                    weighted_sum(i, 2, par, cur)
                    weighted_sum(i, 3, par, cur)

            pe.wait_ge(wqkv_in, 16)
            step(-2, 0, cur=False, pv=False, prev2=False, next1=False)
            pe.wait_ge(consts, 7)
            pe.wait_ge(wqkv_in, 16 * 2)
            step(-1, 1, cur=False, pv=False, prev2=False)
            step(0, 0, pv=False, prev2=False)
            step(1, 1, prev2=False)
            pe.wait_ge(wo_in, 16)
            step(2, 0)
            step(3, 1)
            step(4, 0)
            step(5, 1)
            with pe.Fori(0, (NB - 8) // XS) as t:
                for n in range(XS):
                    step(t * XS + 6 + n, n % 2, slot2=n)
            step(NB - 2, 0, next2=False)
            step(NB - 1, 1, next1=False, next2=False)
            def mean_w2():
                pe.wait_ge(prep, 1)
                pe.wait_ge(exp_done, NB * NC)
                for k in range(HC):
                    mm = nc.tensor.matmul(ps[:, A2, 0:D], mean_ones[:], w2_t[:, k, :],
                                          start=(k == 0), stop=(k == HC - 1))
                mm.then_inc(alpha2_done, 1)

            def turn_y(n):
                pe.wait_ge(ylo_done, n * GB + GB)
                count(pe, yT_ready, n)
                for a in range(2):
                    for k in range(DC):
                        for b in range(GB):
                            at = ((a * DC + k) * GB + b) * P
                            mm = nc.tensor.transpose(ps[:, YT + at // 1024, :].bitcast(F16)[:, at % 1024:at % 1024 + P],
                                                     yparts[:, b, a, P * k:P * k + P], id16[:])
                mm.then_inc(ty_done, 1)

            def hidden(n, k):
                if k == 0:
                    pe.wait_ge(yT_ready, n + 1)
                count(pe, gelu_done, n * HC + k - 3)
                for m, (a, c) in enumerate((a, c) for a in range(2) for c in range(DC)):
                    mm = nc.tensor.matmul(ps[:, HB[k % 4], :], sgn1[:, c, P * k:P * k + P], yT[:, a, c, :, :],
                                          start=(m == 0), stop=(m == 2 * DC - 1))
                mm.then_inc(h_done, 1)

            def second(g, b, par):
                count(pe, zscaled, g * GB + b - 1)
                for m, (k, a) in enumerate((k, a) for k in range(HC) for a in range(2)):
                    if b == 0 and a == 0:
                        pe.wait_ge(hlo_done, g * HC + k + 1)
                    mm = nc.tensor.matmul(ps[:, ZB + b % 2, 0:D], hid[:, par, a, k, P * b:P * b + P], sgn2[:, k, :],
                                          start=(m == 0), stop=(m == 2 * HC - 1))
                mm.then_inc(ffn2_done, 1)

            def group_step(g, par, nxt=True):
                if nxt:
                    turn_y(g + 1)
                for b in range(GB):
                    second(g, b, par)
                    if nxt:
                        hidden(g + 1, 2 * b)
                        hidden(g + 1, 2 * b + 1)

            step(NB, 0, cur=False, next1=False, next2=False, between=mean_w2)
            turn_y(0)
            step(NB + 1, 1, cur=False, pv=False, next1=False, next2=False)
            pe.wait_ge(sgn_ready, 2)
            hidden(0, 0)
            pe.wait_ge(prep, 2)
            pe.wait_ge(onorm_done, NB)
            for k in range(1, HC):
                hidden(0, k)
            pe.wait_ge(resid_done, NB)
            group_step(0, 0)
            with pe.Fori(0, (NG - 2) // 2) as t:
                for k, par in enumerate((1, 0)):
                    group_step(t * 2 + 1 + k, par)
            group_step(NG - 1, 1, nxt=False)

        @block.scalar
        def _(act):
            def step(i, par, cur=True, pv=True, prev2=True, next1=True, next2=True, between=None):
                if prev2:
                    act.wait_ge(pv_done, i - 1)
                    count(act, otok_done, i - 2)
                    nc.scalar.activation(strips[:], ps[:, OT, :].rearrange("p (c t) -> p c t", c=NC),
                                         ACT.Copy).then_inc(strips_ready, 1)
                if between:
                    between()

                def exps(c):
                    act.wait_ge(s_done, i * NC + c + 1)
                    if c == 0:
                        count(act, pv_done, i - 1)
                    nc.scalar.activation(prob[:, par, CH * c:CH * c + CH, :],
                                         ps[:, SC + 2 * (c % 2):SC + 2 * (c % 2) + 2, :],
                                         ACT.Exp, scale=QK_SCALE ** -2).then_inc(exp_done, 1)

                if cur:
                    exps(0)
                    exps(1)
                if next2:
                    act.wait_ge(qkproj_done, i + 3)
                    count(act, ss_done, i + 2)
                    nc.scalar.activation(sq[:], ps[:, QK, :], ACT.Square, scale=1 / QK_SCALE).then_inc(sq_done, 1)
                if cur:
                    act.wait_ge(v_done, i + 1)
                    nc.scalar.activation(vsb[:, par, :, 0:HD],
                                         ps[:, VO, 0:D].rearrange("p (h d) -> p h d", d=HD),
                                         ACT.Copy).then_inc(v_ready, 1)
                    exps(2)
                if prev2:
                    act.wait_ge(ot_done, i - 1)
                    count(act, wo_done, i - 2)
                    nc.scalar.activation(oT[:], ps[:, VO, 0:D].rearrange("p (k t) -> p k t", k=DC),
                                         ACT.Copy).then_inc(ot_ready, 1)
                if cur:
                    exps(3)
                if next1:
                    act.wait_ge(tq_done, i + 2)
                    count(act, s_done, (i + 1) * NC)
                    nc.scalar.activation(qT[:, :, 1 - par, :], tr16.rearrange("p (m t) -> p m t", m=PAIRS),
                                         ACT.Copy).then_inc(q_ready, 1)
                if next2:
                    act.wait_ge(qkn_done, i + 3)
                    count(act, tk_done, i + 1)
                    src = qkn[:].rearrange("p (h d) -> p h d", d=HD)
                    nc.scalar.activation(parts[:, par, 0:H, 0, :], src[:, 0:H, :], ACT.Copy)
                    nc.scalar.activation(parts[:, par, H:2 * H, 0:2, :],
                                         src[:, H:2 * H, :].unsqueeze(2).to_broadcast([P, H, 2, HD]),
                                         ACT.Copy).then_inc(hi_ready, 1)

            act.wait_ge(rel_f, 1)
            for h in range(TH):
                nc.scalar.activation(alibi[:, h, :], rel[:].rearrange("p a b -> p (a b)"), ACT.Exp, scale=-SLOPES[h])
            act.wait_ge(rel_f, 2)
            for h in range(TH, H):
                for a, key in enumerate((rel[:, 0, 0:1], far_key[:])):
                    fac = nc.scalar.activation(fade[:, a, h - TH, :], key.to_broadcast([P, HD + 1]), ACT.Exp,
                                               scale=-SLOPES[h])
            fac.then_inc(alibi_done, 1)
            step(-2, 0, cur=False, pv=False, prev2=False, next1=False)
            act.wait_ge(consts, 7)
            step(-1, 1, cur=False, pv=False, prev2=False)
            step(0, 0, pv=False, prev2=False)
            step(1, 1, prev2=False)
            step(2, 0)
            step(3, 1)
            act.wait_ge(mlp_in, 16 * 5)
            nc.scalar.activation(sgn2[:], w2_t[:], ACT.Sign).then_inc(sgn_ready, 1)
            nc.scalar.activation(sgn1[:], w1_t[:], ACT.Sign).then_inc(sgn_ready, 1)
            with act.Fori(0, (NB - 6) // 2) as t:
                for par in range(2):
                    step(t * 2 + 4 + par, par)
            step(NB - 2, 0, next2=False)
            step(NB - 1, 1, next1=False, next2=False)

            def high_y(n, b):
                act.wait_ge(y_done, n * GB + b + 1)
                count(act, ty_done, n)
                nc.scalar.activation(yparts[:, b, 0, :], resid[:, n * GB + b, :], ACT.Copy).then_inc(yhi_done, 1)

            def take_y(n):
                act.wait_ge(ty_done, n + 1)
                count(act, h_done, n * HC)
                for a in range(2):
                    cp = nc.scalar.activation(yT[:, a, :, :, :].rearrange("p c b t -> p (c b t)"),
                                              ps[:, YT + a, :].bitcast(F16), ACT.Copy)
                cp.then_inc(yT_ready, 1)

            def activate(n, par, nxt=True):
                if not isinstance(n, int) or n > 1:
                    act.wait_ge(ffn2_done, n * GB - GB)
                for b in range(GB):
                    pair = (2 * b, 2 * b + 1)
                    for k in pair:
                        act.wait_ge(h_done, n * HC + k + 1)
                        count(act, hlo_done, n * HC + k - 3)
                        nc.scalar.activation(gelu[:, k % 4, :], ps[:, HB[k % 4], :], ACT.Gelu,
                                             bias=bias1[:, k:k + 1], scale=alpha1[:, k:k + 1]).then_inc(gelu_done, 1)
                    for k in pair:
                        act.wait_ge(gelu_done, n * HC + k + 1)
                        nc.scalar.activation(hid[:, par, 0, k, :], gelu[:, k % 4, :], ACT.Copy,
                                             scale=h_scale[:]).then_inc(hhi_done, 1)
                    if nxt:
                        high_y(n + 1, b)

            def group_step(n, par, nxt=True):
                take_y(n)
                activate(n, par, nxt)

            for b in range(GB):
                high_y(0, b)
            step(NB, 0, cur=False, next1=False, next2=False)
            step(NB + 1, 1, cur=False, pv=False, next1=False, next2=False, between=lambda: take_y(0))
            act.wait_ge(prep, 2)
            activate(0, 0)
            group_step(1, 1)
            with act.Fori(0, (NG - 4) // 2) as t:
                for par in range(2):
                    group_step(t * 2 + 2 + par, par)
            group_step(NG - 2, 0)
            group_step(NG - 1, 1, nxt=False)

        @block.vector
        def _(dve):
            def rsqrt_seed(s, half_, y, eps, op, done, base, scale=1.0):
                nc.vector.tensor_scalar(half_, s, eps, -0.5 / scale ** 2, op, ALU.mult).then_inc(done, 1)
                dve.wait_ge(done, base + 1)
                nc.vector.tensor_scalar(y.bitcast(I32), half_.bitcast(I32), -0.5, SEED_BASE,
                                        ALU.mult, ALU.add).then_inc(done, 1)

            def rsqrt_round(r, half_, a, b, y, done, base):
                dve.wait_ge(done, base + 3 * r + 2)
                nc.vector.tensor_tensor(a, half_, y, ALU.mult).then_inc(done, 1)
                dve.wait_ge(done, base + 3 * r + 3)
                nc.vector.tensor_tensor(b, a, y, ALU.mult).then_inc(done, 1)
                dve.wait_ge(done, base + 3 * r + 4)
                nc.vector.scalar_tensor_tensor(out=y, in0=b, scalar=1.5, in1=y, op0=ALU.add,
                                               op1=ALU.mult).then_inc(done, 1)

            def rsqrt(s, half_, a, b, y, eps, op, done, base, scale=1.0):
                rsqrt_seed(s, half_, y, eps, op, done, base, scale)
                for r in range(3):
                    rsqrt_round(r, half_, a, b, y, done, base)
                dve.wait_ge(done, base + NEWTON_OPS + 1)

            def step(i, par, cur=True, pv=True, prev2=True, next1=True, next2=True, between=None):
                base = (i + 2) * (NEWTON_OPS + 1)
                norm = (half[:], nt_a[:], nt_b[:], rnorm[:], newton, base)
                if cur:
                    dve.wait_ge(exp_done, i * NC + 1)
                    tile = prob[:, par, 0:TH, :]
                    nc.vector.tensor_tensor(tile, tile, alibi[:, :, P * par:P * par + 2 * P],
                                            ALU.mult).then_inc(table_ready, 1)
                if prev2:
                    sums = ps[:, OT, :].rearrange("p (h d) -> p h d", d=32)
                    dve.wait_ge(otok_done, i - 1)
                    count(dve, onorm_done, i - 2)
                    nc.vector.reciprocal(rden[:], sums[:, :, HD]).then_inc(rden_done, 1)
                    dve.wait_ge(rden_done, i - 1)
                    count(dve, ot_done, i - 2)
                    nc.vector.tensor_tensor(otok[:].rearrange("p (h d) -> p h d", d=HD), sums[:, :, 0:HD],
                                            rden[:].unsqueeze(2).to_broadcast([P, H, HD]),
                                            ALU.mult).then_inc(onorm_done, 1)
                if next2:
                    dve.wait_ge(sq_done, i + 3)
                    count(dve, newton, base - NEWTON_OPS)
                    nc.vector.tensor_reduce(ss[:], sq[:].rearrange("p (h d) -> p h d", d=HD), AX.X,
                                            ALU.add).then_inc(ss_done, 1)
                    dve.wait_ge(ss_done, i + 3)
                    count(dve, qkn_done, i + 2)
                    rsqrt_seed(ss[:], half[:], rnorm[:], (NORM_EPS / QK_SCALE) ** 2, ALU.max, newton, base)
                if next1:
                    dve.wait_ge(lo_ready, i + 2)
                    nc.vector.tensor_copy(parts[:, 1 - par, 0:H, 2:4, :],
                                          parts[:, 1 - par, 0:H, 0:2, :]).then_inc(parts_ready, 1)
                if next2:
                    rsqrt_round(0, *norm)
                if cur:
                    dve.wait_ge(v_ready, i + 1)
                    nc.vector.tensor_tensor(vdiag[:, par, :, :], vsb[:, par, TH:H, :], fade[:, 0, :, :],
                                            ALU.mult).then_inc(vdiag_ready, 1)
                    count(dve, pv_done, i - 1)
                    nc.vector.tensor_tensor(vnext[:], vsb[:, par, TH:H, :], fade[:, 1, :, :],
                                            ALU.mult).then_inc(vfade_ready, 1)
                if between:
                    between()
                if next2:
                    rsqrt_round(1, *norm)
                if prev2:
                    dve.wait_ge(wo_done, i - 1)
                    nc.vector.tensor_tensor(resid[:, i - 2, :], resid[:, i - 2, :], ps[:, VO, D:2 * D],
                                            ALU.add).then_inc(resid_done, 1)
                if next2:
                    rsqrt_round(2, *norm)
                if prev2:
                    dve.wait_ge(rel_cut, 3)
                    dve.wait_ge(resid_done, i - 1)
                    count(dve, aggr_done, i - 2)
                    nc.vector.bn_stats(stats[:], resid[:, i - 2, :]).then_inc(stats_done, 1)
                if next2:
                    dve.wait_ge(newton, base + NEWTON_OPS + 1)
                    count(dve, lo_ready, i + 2)
                    nc.vector.tensor_tensor(qkn[:].rearrange("p (h d) -> p h d", d=HD),
                                            ps[:, QK, :].rearrange("p (h d) -> p h d", d=HD),
                                            rnorm[:].unsqueeze(2).to_broadcast([P, 2 * H, HD]),
                                            ALU.mult).then_inc(qkn_done, 1)
                if next1:
                    dve.wait_ge(tk_done, i + 2)
                    count(dve, s_done, (i + 1) * NC)
                    for s in range(2):
                        rows = slice(64 * s, 64 * s + 64)
                        cp = nc.vector.tensor_copy(kTz[rows, s, :, :],
                                                   tr16[rows, :].rearrange("p (m t) -> p m t", m=PAIRS))
                    cp.then_inc(k_ready, 1)
                if prev2:
                    dve.wait_ge(rel_cut, 3)
                    dve.wait_ge(stats_done, i - 1)
                    count(dve, mv_done, i - 2)
                    nc.vector.bn_aggr(mv_new[:], stats[:]).then_inc(aggr_done, 1)
                if prev2:
                    dve.wait_ge(aggr_done, i - 1)
                    nc.vector.tensor_copy(mv[:, i - 2, :], mv_new[:]).then_inc(mv_done, 1)

            dve.wait_ge(rel_cut, 3)
            nc.vector.tensor_copy(rel[:], rel_i[:]).then_inc(rel_f, 1)
            dve.wait_ge(rel_f, 1)
            nc.vector.tensor_scalar(far_key[:], rel[:, 0, 0:1], float(P), None, ALU.add).then_inc(rel_f, 1)
            nc.vector.memset(vsb[:], 1.0).then_inc(consts, 1)
            nc.vector.memset(ps[:, OT, :], 0.0).then_inc(consts, 1)
            nc.vector.memset(mean_ones[:], 1.0 / HID).then_inc(consts, 1)
            dve.wait_ge(alibi_done, 1)
            step(-2, 0, cur=False, pv=False, prev2=False, next1=False)
            step(-1, 1, cur=False, pv=False, prev2=False)
            step(0, 0, pv=False, prev2=False)
            step(1, 1, prev2=False)
            step(2, 0)
            step(3, 1)
            dve.wait_ge(mlp_in, 16 * 5)
            dve.wait_ge(sgn_ready, 1)
            nc.vector.tensor_tensor(w2_t[:], w2_t[:], sgn2[:], ALU.mult).then_inc(prep, 1)
            nc.vector.tensor_reduce(alpha1[:], w1_nat[:], AX.X, ALU.add, apply_absolute_value=True).then_inc(abs_done, 1)
            dve.wait_ge(abs_done, 1)
            nc.vector.scalar_tensor_tensor(out=bound[:], in0=bias1[:], scalar=-1.0, in1=alpha1[:], op0=ALU.mult,
                                           op1=ALU.add).then_inc(abs_done, 1)
            nc.vector.tensor_tensor(hpos[:], bias1[:], alpha1[:], ALU.add).then_inc(abs_done, 1)
            dve.wait_ge(abs_done, 3)
            nc.vector.tensor_tensor(bound[:], bound[:], hpos[:], ALU.max).then_inc(abs_done, 1)
            nc.vector.tensor_scalar(alpha1[:], alpha1[:], 1.0 / (D * Y_SCALE), None, ALU.mult).then_inc(abs_done, 1)
            nc.vector.tensor_scalar(bias2[:], bias2[:], Y_SCALE, None, ALU.mult).then_inc(abs_done, 1)
            dve.wait_ge(abs_done, 6)
            nc.vector.tensor_reduce(bound1[:], bound[:], AX.X, ALU.max).then_inc(bound_done, 1)
            with dve.Fori(0, (NB - 6) // 2) as t:
                for par in range(2):
                    step(t * 2 + 4 + par, par)
            def rstd_of(lo, hi, done):
                dve.wait_ge(mv_done, hi)
                n = hi - lo
                rsqrt(mv[:, lo:hi, 1], half[:, 0:n], nt_a[:, 0:n], nt_b[:, 0:n], rstd[:, lo:hi, 0], LN_EPS, ALU.add,
                      newton, done, Y_SCALE)

            def normalise(m):
                nc.vector.tensor_scalar(resid[:, m, :], resid[:, m, :], mv[:, m, 0:1], rstd[:, m, :],
                                        ALU.subtract, ALU.mult).then_inc(y_done, 1)

            def hidden_low(n, k, par):
                dve.wait_ge(hhi_done, n * HC + k + 1)
                nc.vector.scalar_tensor_tensor(out=hid[:, par, 1, k, :], in0=gelu[:, k % 4, :], scalar=h_scale[:],
                                               in1=hid[:, par, 0, k, :], op0=ALU.mult,
                                               op1=ALU.subtract).then_inc(hlo_done, 1)

            def statistics(g, b, par):
                summed = g * GB + b + 1
                dve.wait_ge(rel_cut, 3)
                dve.wait_ge(zsum, summed)
                count(dve, zaggr, summed - 1)
                nc.vector.bn_stats(zstats[:], z[:, par, b, :]).then_inc(zstat, 1)
                dve.wait_ge(rel_cut, 3)
                dve.wait_ge(zstat, summed)
                if b == 0:
                    count(dve, z_ready, g * GB)
                nc.vector.bn_aggr(zmv[:, b, :], zstats[:]).then_inc(zaggr, 1)

            def finish_group(g, par, nxt=True, nxt2=True):
                if nxt2:
                    normalise((g + 2) * GB)
                for b in range(GB):
                    m = g * GB + b
                    dve.wait_ge(ffn2_done, m + 1)
                    if b == 0:
                        count(dve, stored[par], (g - par) * 8)
                    nc.vector.tensor_tensor(z[:, par, b, :], ps[:, ZB + b % 2, 0:D], alpha2[:],
                                            ALU.mult).then_inc(zscaled, 1)
                    if nxt2 and b < GB - 1:
                        normalise((g + 2) * GB + b + 1)
                    if nxt:
                        for k in (2 * b, 2 * b + 1):
                            hidden_low(g + 1, k, 1 - par)
                    if b > 0:
                        statistics(g, b - 1, par)
                statistics(g, GB - 1, par)
                dve.wait_ge(zaggr, g * GB + GB)
                rsqrt(zmv[:, :, 1], half[:, 0:GB], nt_a[:, 0:GB], nt_b[:, 0:GB], zrstd[:], LN_EPS * Y_SCALE ** 2,
                      ALU.add, znewton, g * (NEWTON_OPS + 1))
                for b in range(GB):
                    nc.vector.tensor_scalar(z[:, par, b, :], z[:, par, b, :], zmv[:, b, 0:1], zrstd[:, b:b + 1],
                                            ALU.subtract, ALU.mult).then_inc(z_ready, 1)

            step(NB - 2, 0, next2=False)
            done = NB * (NEWTON_OPS + 1)

            def early():
                rstd_of(0, EARLY, done)
                for m in range(GB):
                    normalise(m)

            step(NB - 1, 1, next1=False, next2=False, between=early)
            step(NB, 0, cur=False, next1=False, next2=False)
            dve.wait_ge(bound_all, 1)
            nc.vector.tensor_scalar(bound1[:], bound1[:], 1e-30, 2.0 ** -14, ALU.max, ALU.mult).then_inc(abs_done, 1)
            dve.wait_ge(abs_done, 7)
            nc.vector.reciprocal(h_scale[:], bound1[:]).then_inc(abs_done, 1)
            dve.wait_ge(abs_done, 8)
            nc.vector.tensor_scalar(h_scale[:].bitcast(I32), h_scale[:].bitcast(I32), 0x7F800000, None,
                                    ALU.bitwise_and).then_inc(abs_done, 1)
            dve.wait_ge(abs_done, 9)
            nc.vector.tensor_scalar(h_unscale[:].bitcast(I32), h_scale[:].bitcast(I32), -1.0, float(254 << 23),
                                    ALU.mult, ALU.add).then_inc(abs_done, 1)
            dve.wait_ge(abs_done, 10)
            dve.wait_ge(alpha2_done, 1)
            nc.vector.tensor_scalar(alpha2[:], ps[:, A2, 0:D], h_unscale[:], Y_SCALE, ALU.mult, ALU.mult).then_inc(prep, 1)
            for b in range(GB):
                normalise(GB + b)
            step(NB + 1, 1, cur=False, pv=False, next1=False, next2=False)
            for k in range(HC):
                hidden_low(0, k, 0)
            for par in range(2):
                finish_group(par, par)
                if par == 0:
                    rstd_of(EARLY, NB, done + NEWTON_OPS + 1)
            with dve.Fori(0, (NG - 4) // 2) as t:
                for par in range(2):
                    finish_group(t * 2 + 2 + par, par)
            finish_group(NG - 2, 0, nxt2=False)
            finish_group(NG - 1, 1, nxt=False, nxt2=False)

        @block.gpsimd
        def _(pool):
            for a in range(3):
                nc.gpsimd.iota(rel_i[:, a, :], pattern=[[-1, P]], base=P * (a % 2),
                               channel_multiplier=1).then_inc(rel_made, 1)
            nc.gpsimd.memset(id16[:], 0.0).then_inc(id_zero, 1)
            nc.gpsimd.memset(id32[:], 0.0).then_inc(id_zero, 1)
            pool.wait_ge(rel_made, 3)
            for a in range(3):
                near = a % 2
                nc.gpsimd.affine_select(out=rel_i[:, a, :], in_=rel_i[:, a, :], compare_op=ALU.is_ge, fill=FAR,
                                        base=-near, pattern=[[1 if near else -1, P]],
                                        channel_multiplier=-1 if near else 1).then_inc(rel_cut, 1)
            pool.wait_ge(id_zero, 2)
            for m in (id16, id32):
                nc.gpsimd.affine_select(out=m[:], in_=m[:], compare_op=ALU.not_equal, fill=1.0, base=0,
                                        pattern=[[-1, P]], channel_multiplier=1).then_inc(consts, 1)
            nc.gpsimd.memset(qT[:], 0.0).then_inc(consts, 1)
            nc.gpsimd.memset(kTz[:], 0.0).then_inc(consts, 1)

            def low_part(n, par):
                pool.wait_ge(hi_ready, n + 1)
                src = qkn[:].rearrange("p (h d) -> p h d", d=HD)
                nc.gpsimd.tensor_tensor(parts[:, par, 0:H, 1, :], src[:, 0:H, :], parts[:, par, 0:H, 0, :],
                                        ALU.subtract)
                nc.gpsimd.tensor_tensor(parts[:, par, H:2 * H, 2:4, :],
                                        src[:, H:2 * H, :].unsqueeze(2).to_broadcast([P, H, 2, HD]),
                                        parts[:, par, H:2 * H, 0:2, :], ALU.subtract).then_inc(lo_ready, 1)

            def cut_chunk(i, c, par):
                chunks = pool.to_reg(i * NC + c + 1)
                pool.wait_ge(alibi_done, 1)
                pool.wait_ge(exp_done, chunks)
                for near, tile in enumerate((par, 1 - par)):
                    at = prob[:, par, CH * c:CH * c + CH, P * tile:P * tile + P]
                    sel = nc.gpsimd.affine_select(out=at, in_=at, compare_op=ALU.is_ge, fill=0.0, base=-near,
                                                  pattern=[[0, CH], [1 if near else -1, P]],
                                                  channel_multiplier=-1 if near else 1)
                sel.then_inc(cut_ready, 1)

            def step(i, par, next2=True):
                for c in range(1, NC):
                    cut_chunk(i, c, par)
                if next2:
                    low_part(i + 2, par)

            low_part(0, 0)
            low_part(1, 1)
            with pool.Fori(0, (NB - 2) // 2) as t:
                for par in range(2):
                    step(t * 2 + par, par)
            step(NB - 2, 0, next2=False)
            step(NB - 1, 1, next2=False)

            pool.wait_ge(bound_done, 1)
            nc.gpsimd.partition_all_reduce(bound1[:], bound1[:], P, bass.bass_isa.ReduceOp.max).then_inc(bound_all, 1)

            def low_y(n, b):
                m = n * GB + b
                blocks = m + 1
                pool.wait_ge(alibi_done, 1)
                pool.wait_ge(yhi_done, blocks)
                nc.gpsimd.tensor_tensor(yparts[:, b, 1, :], resid[:, m, :], yparts[:, b, 0, :],
                                        ALU.subtract).then_inc(ylo_done, 1)
                pool.wait_ge(alibi_done, 1)
                pool.wait_ge(ylo_done, blocks)
                nc.gpsimd.tensor_tensor(resid[:, m, :], resid[:, m, :], bias2[:], ALU.add).then_inc(yb_done, 1)

            def group_step(g, par, nxt2=True):
                for b in range(GB):
                    m = g * GB + b
                    summed = m + 1
                    pool.wait_ge(alibi_done, 1)
                    pool.wait_ge(yb_done, summed)
                    pool.wait_ge(zscaled, summed)
                    nc.gpsimd.tensor_tensor(z[:, par, b, :], z[:, par, b, :], resid[:, m, :],
                                            ALU.add).then_inc(zsum, 1)
                    if nxt2:
                        low_y(g + 2, b)

            for n in range(2):
                for b in range(GB):
                    low_y(n, b)
            with pool.Fori(0, (NG - 2) // 2) as t:
                for par in range(2):
                    group_step(t * 2 + par, par)
            group_step(NG - 2, 0, nxt2=False)
            group_step(NG - 1, 1, nxt2=False)


_OUT = "out_dram"


def kernel(L0_attn_x, L0_attn_Wq, L0_attn_Wk, L0_attn_Wv, L0_attn_Wo, L0_ffn_w1, L0_ffn_b1, L0_ffn_w2, L0_ffn_b2):
    import concourse.bacc as bacc
    from concourse.bass_utils import run_bass_kernel_spmd

    def cont(a):
        return np.ascontiguousarray(a)

    x = np.asarray(L0_attn_x).reshape(NB, P, D)
    wqkv = np.concatenate([np.asarray(w) for w in (L0_attn_Wq, L0_attn_Wk, L0_attn_Wv)], axis=0)
    arrays = {
        "x": cont(x),
        "xT": cont(x.reshape(NB, P, DC, P).transpose(0, 3, 2, 1)),
        "wqkvT": cont(wqkv.T.reshape(DC, P, 3 * D).transpose(1, 0, 2)),
        "woT": cont(np.asarray(L0_attn_Wo).T.reshape(DC, P, D).transpose(1, 0, 2)),
        "w1": cont(np.asarray(L0_ffn_w1).reshape(HC, P, D).transpose(1, 0, 2)),
        "w1T": cont(np.asarray(L0_ffn_w1).T.reshape(DC, P, HID).transpose(1, 0, 2)),
        "b1c": cont(np.asarray(L0_ffn_b1).reshape(HC, P).T),
        "w2T": cont(np.asarray(L0_ffn_w2).T.reshape(HC, P, D).transpose(1, 0, 2)),
        "b2": cont(np.broadcast_to(np.asarray(L0_ffn_b2), (P, D))),
    }
    nc = bacc.Bacc("TRN2", target_bir_lowering=False, num_devices=1)
    args = [nc.dram_tensor(f"in_{n}", a.shape, F32, kind="ExternalInput").ap() for n, a in arrays.items()]
    out = nc.dram_tensor(_OUT, (T, D), F32, kind="ExternalOutput").ap()
    build(nc, *args, out.rearrange("(g b p) d -> g p b d", b=GB, p=P))
    r = run_bass_kernel_spmd(nc, [{f"in_{n}": a for n, a in arrays.items()}], core_ids=[0])
    return r.results[0][_OUT].reshape(1, T, D)
```

```python
from contextlib import ExitStack

import numpy as np

import concourse.bass as bass
from concourse import mybir

F32 = mybir.dt.float32
F16 = mybir.dt.float16
I32 = mybir.dt.int32
ALU = mybir.AluOpType
ACT = mybir.ActivationFunctionType
AX = mybir.AxisListType

P = 128
D = 256
DC = D // P
T = 4096
NB = T // P
H = 16
HD = D // H
XS = 4
PAIRS = H // 2
CH = 4
NC = H // CH
HID = 1024
HC = HID // P
GB = 4
NG = NB // GB
QK_SCALE = 2.0 ** 10
Y_SCALE = 2.0 ** 11
NORM_EPS = 1e-6
LN_EPS = 1e-5
TH = CH
FAR = 1.0e5
SLOPES = [2.0 ** (-8.0 * h / (H - 1)) for h in range(H)]
SEED_BASE = float(0x5F3759DF - (1 << 22) - (1 << 30))
NEWTON_OPS = 10


def count(sem_engine, sem, value):
    if isinstance(value, int) and value <= 0:
        return
    sem_engine.wait_ge(sem, value)


def build(nc, x, xT, wqkvT, woT, w1, w1T, b1c, w2T, b2, out):
    with ExitStack() as ctx:
        def sb(name, shape, dt=F32):
            return ctx.enter_context(nc.sbuf_tensor(name, shape, dt))

        def sem(name):
            return ctx.enter_context(nc.semaphore(name))

        wqkv = sb("wqkv", [P, DC, 3 * D])
        wo = sb("wo", [P, DC, D])
        w1_nat = sb("w1_nat", [P, HC, D])
        w1_t = sb("w1_t", [P, DC, HID])
        w2_t = sb("w2_t", [P, HC, D])
        sgn1 = sb("sgn1", [P, DC, HID], F16)
        sgn2 = sb("sgn2", [P, HC, D], F16)
        bias1 = sb("bias1", [P, HC])
        bias2 = sb("bias2", [P, D])
        alpha1 = sb("alpha1", [P, HC])
        alpha2 = sb("alpha2", [P, D])
        mean_ones = sb("mean_ones", [P, P])
        id16 = sb("id16", [P, P], F16)
        id32 = sb("id32", [P, P])
        rel_i = sb("rel_i", [P, 3, P], I32)
        rel = sb("rel", [P, 3, P])
        alibi = sb("alibi", [P, TH, 3 * P])
        far_key = sb("far_key", [P, 1])
        fade = sb("fade", [P, 2, H - TH, HD + 1])
        xt = sb("xt", [P, XS, DC, P])
        resid = sb("resid", [P, NB, D])
        sq = sb("sq", [P, 2 * D])
        ss = sb("ss", [P, 2 * H])
        half = sb("half", [P, 2 * H + 1])
        nt_a = sb("nt_a", [P, 2 * H + 1])
        nt_b = sb("nt_b", [P, 2 * H + 1])
        rnorm = sb("rnorm", [P, 2 * H + 1])
        qkn = sb("qkn", [P, 2 * D])
        parts = sb("parts", [P, 2, 2 * H, 4, HD], F16)
        qT = sb("qT", [P, PAIRS, 2, P], F16)
        kTz = sb("kTz", [P, 2, PAIRS, P], F16)
        vsb = sb("vsb", [P, 2, H, HD + 1])
        vdiag = sb("vdiag", [P, 2, H - TH, HD + 1])
        vnext = sb("vnext", [P, H - TH, HD + 1])
        prob = sb("prob", [P, 2, H, 2 * P])
        strips = sb("strips", [P, CH, P])
        rden = sb("rden", [P, H])
        otok = sb("otok", [P, D])
        oT = sb("oT", [P, DC, P])
        stats = sb("stats", [P, 6])
        mv = sb("mv", [P, 2])
        yparts = sb("yparts", [P, GB, 2, D], F16)
        yT = sb("yT", [P, 2, 2, DC, GB, P], F16)
        gelu = sb("gelu", [P, 4, GB * P])
        hid = prob[:].rearrange("p s h c -> p s (h c)").bitcast(F16).rearrange("p s (a k n) -> p s a k n", a=2, k=HC)
        bound = sb("bound", [P, HC])
        hpos = sb("hpos", [P, HC])
        bound1 = sb("bound1", [P, 1])
        h_scale = sb("h_scale", [P, 1])
        h_unscale = sb("h_unscale", [P, 1])
        z = sb("z", [P, 2, GB, D])
        zstats = sb("zstats", [P, 6])
        zmv = sb("zmv", [P, GB, 2])
        zrstd = sb("zrstd", [P, GB])

        ps = ctx.enter_context(nc.psum_tensor("ps", [P, 8, 512], F32))
        QK, VO, TR, SC, OT = 0, 1, 2, 3, 7
        tr16 = ps[:, TR, :].bitcast(F16)
        YT, ZB, A2 = 3, 0, 6
        HB = (5, 6, 2, 7)
        ZBANKS, LAST_ZBANKS = (ZB, ZB + 1, ZB, ZB + 1), (ZB, ZB + 1, YT, YT + 1)

        x_in = [sem(f"x_in_{n}") for n in range(XS)]
        wqkv_in, wo_in = sem("wqkv_in"), sem("wo_in")
        w2_in, w1_in, mlp_in = sem("w2_in"), sem("w1_in"), sem("mlp_in")
        consts = sem("consts")
        id_zero, rel_made, rel_cut, rel_f = sem("id_zero"), sem("rel_made"), sem("rel_cut"), sem("rel_f")
        alibi_done = sem("alibi_done")
        qkproj_done, sq_done, ss_done, newton, qkn_done = (
            sem(n) for n in ("qkproj_done", "sq_done", "ss_done", "newton", "qkn_done"))
        hi_ready, lo_ready, parts_ready = sem("hi_ready"), sem("lo_ready"), sem("parts_ready")
        tq_done, q_ready, tk_done, k_ready = (sem(n) for n in ("tq_done", "q_ready", "tk_done", "k_ready"))
        v_done, v_ready, vdiag_ready, vfade_ready = (sem(n) for n in ("v_done", "v_ready", "vdiag_ready", "vfade_ready"))
        s_done, exp_done = sem("s_done"), sem("exp_done")
        table_ready, cut_ready = sem("table_ready"), sem("cut_ready")
        pv_done, strips_ready, otok_done = sem("pv_done"), sem("strips_ready"), sem("otok_done")
        rden_done, onorm_done = sem("rden_done"), sem("onorm_done")
        ot_done, ot_ready, wo_done = sem("ot_done"), sem("ot_ready"), sem("wo_done")
        resid_done, stats_done, aggr_done, ln_seed = (
            sem(n) for n in ("resid_done", "stats_done", "aggr_done", "ln_seed"))
        prep = sem("prep")
        sgn_ready = sem("sgn_ready")
        alpha2_done, abs_done = sem("alpha2_done"), sem("abs_done")
        bound_done, bound_all = sem("bound_done"), sem("bound_all")
        y_done, yhi_done, ylo_done, yb_done = (sem(n) for n in ("y_done", "yhi_done", "ylo_done", "yb_done"))
        hhi_first = sem("hhi_first")
        ty_done, yT_ready = sem("ty_done"), sem("yT_ready")
        h_done, gelu_done, hhi_done, hlo_done = (sem(n) for n in ("h_done", "gelu_done", "hhi_done", "hlo_done"))
        ffn2_done = sem("ffn2_done")
        zscaled, zsum, zstat, zaggr = (sem(n) for n in ("zscaled", "zsum", "zstat", "zaggr"))
        znewton, z_ready = sem("znewton"), sem("z_ready")
        stored = [sem("stored_even"), sem("stored_odd")]

        block = ctx.enter_context(nc.Block())

        @block.sync
        def _(sp):
            def load_block(n, slot):
                count(sp, v_done, n - XS + 1)
                sp.dma_start(xt[:, slot], xT[n]).then_inc(x_in[slot], 16)
                sp.dma_start(resid[:, n, :], x[n]).then_inc(x_in[slot], 16)

            sp.dma_start(wqkv[:, :, 0:2 * D], wqkvT[:, :, 0:2 * D]).then_inc(wqkv_in, 16)
            for n in range(XS):
                load_block(n, n)
            sp.dma_start(wqkv[:, :, 2 * D:3 * D], wqkvT[:, :, 2 * D:3 * D]).then_inc(wqkv_in, 16)
            sp.dma_start(wo[:], woT).then_inc(wo_in, 16)
            sp.dma_start(w1_nat[:], w1).then_inc(w1_in, 16)
            sp.dma_start(w2_t[:], w2T).then_inc(w2_in, 16)
            for dst, src in ((w1_t, w1T), (bias1, b1c), (bias2, b2)):
                sp.dma_start(dst[:], src).then_inc(mlp_in, 16)
            with sp.Fori(0, NB // XS - 1) as t:
                for slot in range(XS):
                    load_block(t * XS + XS + slot, slot)

            def store_group(g, par):
                sp.wait_ge(z_ready, g * GB + GB)
                sp.dma_start(out[g], z[:, par]).then_inc(stored[par], 16)

            with sp.Fori(0, NG // 2) as t:
                for par in range(2):
                    store_group(t * 2 + par, par)
            for par in range(2):
                sp.wait_ge(stored[par], 16 * NG // 2)

        @block.tensor
        def _(pe):
            def scores(i, c, par):
                pe.wait_ge(k_ready, i + 1)
                count(pe, exp_done, i * NC + c - 1)
                for j in range(CH):
                    h = CH * c + j
                    mm = nc.tensor.matmul(ps[:, SC + 2 * (c % 2) + j // 2, 256 * (j % 2):256 * (j % 2) + 256],
                                          kTz[:, h % 2, h // 2, :], qT[:, h // 2, :, :], start=True, stop=True)
                mm.then_inc(s_done, 1)

            def weighted_sum(i, c, par, cur):
                if c == 0:
                    pe.wait_ge(v_ready, i + 1 if cur else NB)
                    pe.wait_ge(table_ready, i + 1 if cur else NB)
                    count(pe, onorm_done, i - 1)
                elif c == 1:
                    pe.wait_ge(vfade_ready, i + 1 if cur else NB)
                if c > 0:
                    pe.wait_ge(cut_ready, i * (NC - 1) + c if cur else NB * (NC - 1))
                tiles = [1 - par, par] if cur else [1 - par]
                for n, s in enumerate(tiles):
                    for j in range(CH):
                        h = CH * c + j
                        if c == 0:
                            v = vsb[:, s, h, :]
                        else:
                            v = vdiag[:, s, h - TH, :] if n == 0 else vnext[:, h - TH, :]
                        mm = nc.tensor.matmul(ps[32 * j:32 * j + HD + 1, OT, P * c:P * c + P], v,
                                              prob[:, s, h, P * (1 - par):P * (1 - par) + P],
                                              start=(n == 0), stop=(n == len(tiles) - 1))
                if c == NC - 1:
                    mm.then_inc(pv_done, 1)

            def step(i, par, cur=True, pv=True, prev2=True, next1=True, next2=True, slot2=None, between=None):
                if slot2 is None:
                    slot2 = (i + 2) % XS
                if cur:
                    scores(i, 0, par)
                    scores(i, 1, par)
                if prev2:
                    pe.wait_ge(strips_ready, i - 1)
                    for c in range(NC):
                        mm = nc.tensor.transpose(ps[:, OT, P * c:P * c + P], strips[:, c, :], id32[:])
                    mm.then_inc(otok_done, 1)
                if between:
                    between()
                if next2:
                    pe.wait_ge(x_in[slot2], (i + 2 - slot2) * (32 // XS) + 32)
                    count(pe, qkn_done, i + 2)
                    for k in range(DC):
                        mm = nc.tensor.matmul(ps[:, QK, :], xt[:, slot2, k, :], wqkv[:, k, 0:2 * D],
                                              start=(k == 0), stop=(k == DC - 1))
                    mm.then_inc(qkproj_done, 1)
                if cur:
                    scores(i, 2, par)
                if prev2:
                    pe.wait_ge(onorm_done, i - 1)
                    pe.wait_ge(v_ready, i + 1 if cur else NB)
                    for k in range(DC):
                        mm = nc.tensor.transpose(ps[:, VO, P * k:P * k + P], otok[:, P * k:P * k + P], id32[:])
                    mm.then_inc(ot_done, 1)
                if cur:
                    scores(i, 3, par)
                if next1:
                    pe.wait_ge(parts_ready, i + 2)
                    count(pe, k_ready, i + 1)
                    for m in range(PAIRS):
                        src = parts[:, 1 - par, 2 * m:2 * m + 2, :, :].rearrange("p h a d -> p (h a d)")
                        mm = nc.tensor.transpose(tr16[:, P * m:P * m + P], src, id16[:])
                    mm.then_inc(tq_done, 1)
                if prev2:
                    pe.wait_ge(ot_ready, i - 1)
                    for k in range(DC):
                        mm = nc.tensor.matmul(ps[:, VO, D:2 * D], oT[:, k, :], wo[:, k, :],
                                              start=(k == 0), stop=(k == DC - 1))
                    mm.then_inc(wo_done, 1)
                if pv:
                    weighted_sum(i, 0, par, cur)
                    weighted_sum(i, 1, par, cur)
                if next1:
                    pe.wait_ge(q_ready, i + 2)
                    for m in range(PAIRS):
                        src = parts[:, 1 - par, H + 2 * m:H + 2 * m + 2, :, :].rearrange("p h a d -> p (h a d)")
                        mm = nc.tensor.transpose(tr16[:, P * m:P * m + P], src, id16[:])
                    mm.then_inc(tk_done, 1)
                    if prev2:
                        pe.wait_ge(resid_done, i - 1)
                    count(pe, v_ready, i + 1)
                    for k in range(DC):
                        mm = nc.tensor.matmul(ps[:, VO, 0:D], xt[:, (slot2 - 1) % XS, k, :], wqkv[:, k, 2 * D:3 * D],
                                              start=(k == 0), stop=(k == DC - 1))
                    mm.then_inc(v_done, 1)
                if pv:
                    weighted_sum(i, 2, par, cur)
                    weighted_sum(i, 3, par, cur)

            pe.wait_ge(wqkv_in, 16)
            step(-2, 0, cur=False, pv=False, prev2=False, next1=False)
            pe.wait_ge(consts, 7)
            pe.wait_ge(wqkv_in, 16 * 2)
            step(-1, 1, cur=False, pv=False, prev2=False)
            step(0, 0, pv=False, prev2=False)
            step(1, 1, prev2=False)
            pe.wait_ge(wo_in, 16)
            step(2, 0)
            step(3, 1)
            step(4, 0)
            step(5, 1)
            with pe.Fori(0, (NB - 8) // XS) as t:
                for n in range(XS):
                    step(t * XS + 6 + n, n % 2, slot2=n)
            step(NB - 2, 0, next2=False)
            step(NB - 1, 1, next1=False, next2=False)
            def mean_w2():
                pe.wait_ge(prep, 1)
                pe.wait_ge(exp_done, NB * NC)
                for k in range(HC):
                    mm = nc.tensor.matmul(ps[:, A2, 0:D], mean_ones[:], w2_t[:, k, :],
                                          start=(k == 0), stop=(k == HC - 1))
                mm.then_inc(alpha2_done, 1)

            def turn_y(n):
                pe.wait_ge(ylo_done, n * GB + GB)
                count(pe, yT_ready, 2 * n)
                for a in range(2):
                    for k in range(DC):
                        for b in range(GB):
                            at = ((a * DC + k) * GB + b) * P
                            mm = nc.tensor.transpose(ps[:, YT + at // 1024, :].bitcast(F16)[:, at % 1024:at % 1024 + P],
                                                     yparts[:, b, a, P * k:P * k + P], id16[:])
                mm.then_inc(ty_done, 1)

            def hidden(n, k, par):
                count(pe, gelu_done, n * HC + k - 3)
                for m, (a, c) in enumerate((a, c) for a in range(2) for c in range(DC)):
                    if k == 0 and c == 0:
                        pe.wait_ge(yT_ready, 2 * n + a + 1)
                    mm = nc.tensor.matmul(ps[:, HB[k % 4], :], sgn1[:, c, P * k:P * k + P], yT[:, par, a, c, :, :],
                                          start=(m == 0), stop=(m == 2 * DC - 1))
                mm.then_inc(h_done, 1)

            def second(g, b, par, banks=ZBANKS):
                if b < 2 or banks is ZBANKS:
                    count(pe, zscaled, g * GB + b - 1)
                for m, (k, a) in enumerate((k, a) for k in range(HC) for a in range(2)):
                    if b == 0 and a == 0:
                        pe.wait_ge(hlo_done, g * HC + k + 1)
                    mm = nc.tensor.matmul(ps[:, banks[b], 0:D], hid[:, par, a, k, P * b:P * b + P], sgn2[:, k, :],
                                          start=(m == 0), stop=(m == 2 * HC - 1))
                mm.then_inc(ffn2_done, 1)

            def group_step(g, par, nxt=True, nxt2=True):
                for b in range(GB):
                    if nxt:
                        hidden(g + 1, 2 * b, 1 - par)
                        hidden(g + 1, 2 * b + 1, 1 - par)
                    second(g, b, par, ZBANKS if nxt else LAST_ZBANKS)
                    if nxt2 and b == GB - 2:
                        turn_y(g + 2)

            step(NB, 0, cur=False, next1=False, next2=False, between=mean_w2)
            turn_y(0)
            step(NB + 1, 1, cur=False, pv=False, next1=False, next2=False)
            pe.wait_ge(sgn_ready, 2)
            hidden(0, 0, 0)
            pe.wait_ge(prep, 2)
            pe.wait_ge(onorm_done, NB)
            for k in range(1, HC):
                if k == HC - 2:
                    turn_y(1)
                hidden(0, k, 0)
            pe.wait_ge(resid_done, NB)
            group_step(0, 0)
            group_step(1, 1)
            with pe.Fori(0, (NG - 4) // 2) as t:
                for par in range(2):
                    group_step(t * 2 + 2 + par, par)
            group_step(NG - 2, 0, nxt2=False)
            group_step(NG - 1, 1, nxt=False, nxt2=False)

        @block.scalar
        def _(act):
            def step(i, par, cur=True, pv=True, prev2=True, next1=True, next2=True, between=None, aside=None):
                if prev2:
                    act.wait_ge(pv_done, i - 1)
                    count(act, otok_done, i - 2)
                    nc.scalar.activation(strips[:], ps[:, OT, :].rearrange("p (c t) -> p c t", c=NC),
                                         ACT.Copy).then_inc(strips_ready, 1)
                if between:
                    between()

                def exps(c):
                    act.wait_ge(s_done, i * NC + c + 1)
                    if c == 0:
                        count(act, pv_done, i - 1)
                    nc.scalar.activation(prob[:, par, CH * c:CH * c + CH, :],
                                         ps[:, SC + 2 * (c % 2):SC + 2 * (c % 2) + 2, :],
                                         ACT.Exp, scale=QK_SCALE ** -2).then_inc(exp_done, 1)

                if cur:
                    act.wait_ge(v_done, i + 1)
                    count(act, pv_done, i - 1)
                    nc.scalar.activation(vsb[:, par, :, 0:HD],
                                         ps[:, VO, 0:D].rearrange("p (h d) -> p h d", d=HD),
                                         ACT.Copy).then_inc(v_ready, 1)
                    exps(0)
                    exps(1)
                if next2:
                    act.wait_ge(qkproj_done, i + 3)
                    count(act, ss_done, i + 2)
                    nc.scalar.activation(sq[:], ps[:, QK, :], ACT.Square, scale=1 / QK_SCALE).then_inc(sq_done, 1)
                if prev2:
                    act.wait_ge(ot_done, i - 1)
                    count(act, wo_done, i - 2)
                    nc.scalar.activation(oT[:], ps[:, VO, 0:D].rearrange("p (k t) -> p k t", k=DC),
                                         ACT.Copy).then_inc(ot_ready, 1)
                if cur:
                    exps(2)
                if cur:
                    exps(3)
                if next1:
                    act.wait_ge(tq_done, i + 2)
                    count(act, s_done, (i + 1) * NC)
                    nc.scalar.activation(qT[:, :, 1 - par, :], tr16.rearrange("p (m t) -> p m t", m=PAIRS),
                                         ACT.Copy).then_inc(q_ready, 1)
                if aside:
                    aside()
                if next2:
                    act.wait_ge(qkn_done, i + 3)
                    count(act, tk_done, i + 1)
                    src = qkn[:].rearrange("p (h d) -> p h d", d=HD)
                    nc.scalar.activation(parts[:, par, 0:H, 0, :], src[:, 0:H, :], ACT.Copy)
                    nc.scalar.activation(parts[:, par, H:2 * H, 0:2, :],
                                         src[:, H:2 * H, :].unsqueeze(2).to_broadcast([P, H, 2, HD]),
                                         ACT.Copy).then_inc(hi_ready, 1)

            act.wait_ge(rel_f, 1)
            for h in range(TH):
                nc.scalar.activation(alibi[:, h, :], rel[:].rearrange("p a b -> p (a b)"), ACT.Exp, scale=-SLOPES[h])
            act.wait_ge(rel_f, 2)
            for h in range(TH, H):
                for a, key in enumerate((rel[:, 0, 0:1], far_key[:])):
                    fac = nc.scalar.activation(fade[:, a, h - TH, :], key.to_broadcast([P, HD + 1]), ACT.Exp,
                                               scale=-SLOPES[h])
            fac.then_inc(alibi_done, 1)
            def signs2():
                act.wait_ge(w2_in, 16)
                nc.scalar.activation(sgn2[:], w2_t[:], ACT.Sign).then_inc(sgn_ready, 1)

            def signs1():
                act.wait_ge(mlp_in, 16 * 3)
                nc.scalar.activation(sgn1[:], w1_t[:], ACT.Sign).then_inc(sgn_ready, 1)

            step(-2, 0, cur=False, pv=False, prev2=False, next1=False)
            act.wait_ge(consts, 7)
            step(-1, 1, cur=False, pv=False, prev2=False, aside=signs2)
            step(0, 0, pv=False, prev2=False)
            step(1, 1, prev2=False, aside=signs1)
            step(2, 0)
            step(3, 1)
            with act.Fori(0, (NB - 6) // 2) as t:
                for par in range(2):
                    step(t * 2 + 4 + par, par)
            step(NB - 2, 0, next2=False)
            step(NB - 1, 1, next1=False, next2=False)

            def high_y(n, b):
                act.wait_ge(y_done, n * GB + b + 1)
                count(act, ty_done, n)
                nc.scalar.activation(yparts[:, b, 0, :], resid[:, n * GB + b, :], ACT.Copy).then_inc(yhi_done, 1)

            def take_y(n, par, part):
                act.wait_ge(ty_done, n + 1)
                if part == 0 and (not isinstance(n, int) or n > 1):
                    act.wait_ge(h_done, n * HC - HC)
                nc.scalar.activation(yT[:, par, part, :, :, :].rearrange("p c b t -> p (c b t)"),
                                     ps[:, YT + part, :].bitcast(F16), ACT.Copy).then_inc(yT_ready, 1)

            def activate(n, par, nxt=True, first=False):
                if not isinstance(n, int) or n > 1:
                    act.wait_ge(ffn2_done, n * GB - GB)
                for b in range(GB):
                    pair = (2 * b, 2 * b + 1)
                    for k in pair:
                        act.wait_ge(h_done, n * HC + k + 1)
                        count(act, hlo_done, n * HC + k - 3)
                        nc.scalar.activation(gelu[:, k % 4, :], ps[:, HB[k % 4], :], ACT.Gelu,
                                             bias=bias1[:, k:k + 1], scale=alpha1[:, k:k + 1]).then_inc(gelu_done, 1)
                    if nxt and b == GB - 1:
                        take_y(n + 1, 1 - par, 1)
                    for k in () if first else pair:
                        act.wait_ge(gelu_done, n * HC + k + 1)
                        nc.scalar.activation(hid[:, par, 0, k, :], gelu[:, k % 4, :], ACT.Copy,
                                             scale=h_scale[:]).then_inc(hhi_done, 1)
                    if nxt and not first and b < GB // 2:
                        high_y(n + 1, 2 * b)
                        high_y(n + 1, 2 * b + 1)
                    if nxt and b == GB - 2:
                        take_y(n + 1, 1 - par, 0)

            def take_first():
                for part in range(2):
                    take_y(0, 0, part)

            for b in range(GB):
                high_y(0, b)
            step(NB, 0, cur=False, next1=False, next2=False)
            step(NB + 1, 1, cur=False, pv=False, next1=False, next2=False, between=take_first)
            for b in range(GB):
                high_y(1, b)
            act.wait_ge(prep, 2)
            activate(0, 0, first=True)
            activate(1, 1)
            with act.Fori(0, (NG - 4) // 2) as t:
                for par in range(2):
                    activate(t * 2 + 2 + par, par)
            activate(NG - 2, 0)
            activate(NG - 1, 1, nxt=False)

        @block.vector
        def _(dve):
            def rsqrt_seed(s, half_, eps, op, done, scale=1.0):
                nc.vector.tensor_scalar(half_, s, eps, -0.5 / scale ** 2, op, ALU.mult).then_inc(done, 1)

            def rsqrt_guess(half_, y, done, base):
                dve.wait_ge(done, base + 1)
                nc.vector.tensor_scalar(y.bitcast(I32), half_.bitcast(I32), -0.5, SEED_BASE,
                                        ALU.mult, ALU.add).then_inc(done, 1)

            def rsqrt_round(r, half_, a, b, y, done, base):
                dve.wait_ge(done, base + 3 * r + 2)
                nc.vector.tensor_tensor(a, half_, y, ALU.mult).then_inc(done, 1)
                dve.wait_ge(done, base + 3 * r + 3)
                nc.vector.tensor_tensor(b, a, y, ALU.mult).then_inc(done, 1)
                dve.wait_ge(done, base + 3 * r + 4)
                nc.vector.scalar_tensor_tensor(out=y, in0=b, scalar=1.5, in1=y, op0=ALU.add,
                                               op1=ALU.mult).then_inc(done, 1)

            def rsqrt(s, half_, a, b, y, eps, op, done, base, scale=1.0):
                rsqrt_seed(s, half_, eps, op, done, scale)
                rsqrt_guess(half_, y, done, base)
                for r in range(3):
                    rsqrt_round(r, half_, a, b, y, done, base)
                dve.wait_ge(done, base + NEWTON_OPS + 1)

            def step(i, par, cur=True, pv=True, prev2=True, next1=True, next2=True, prev3=True, aside=None):
                base = (i + 2) * (NEWTON_OPS + 1)
                if not next2:
                    base = NB * (NEWTON_OPS + 1) + (i - NB + 2) * NEWTON_OPS - 1
                cols = slice(0 if next2 else 2 * H, 2 * H + 1 if prev3 else 2 * H)
                norm = (half[:, cols], nt_a[:, cols], nt_b[:, cols], rnorm[:, cols], newton, base)
                rounds = next2 or prev3
                if cur:
                    dve.wait_ge(v_ready, i + 1)
                    nc.vector.tensor_tensor(vdiag[:, par, :, :], vsb[:, par, TH:H, :], fade[:, 0, :, :],
                                            ALU.mult).then_inc(vdiag_ready, 1)
                    count(dve, pv_done, i - 1)
                    nc.vector.tensor_tensor(vnext[:], vsb[:, par, TH:H, :], fade[:, 1, :, :],
                                            ALU.mult).then_inc(vfade_ready, 1)
                if prev2:
                    sums = ps[:, OT, :].rearrange("p (h d) -> p h d", d=32)
                    dve.wait_ge(otok_done, i - 1)
                    count(dve, onorm_done, i - 2)
                    nc.vector.reciprocal(rden[:], sums[:, :, HD]).then_inc(rden_done, 1)
                    dve.wait_ge(rden_done, i - 1)
                    count(dve, ot_done, i - 2)
                    nc.vector.tensor_tensor(otok[:].rearrange("p (h d) -> p h d", d=HD), sums[:, :, 0:HD],
                                            rden[:].unsqueeze(2).to_broadcast([P, H, HD]),
                                            ALU.mult).then_inc(onorm_done, 1)
                if cur:
                    dve.wait_ge(exp_done, i * NC + 1)
                    tile = prob[:, par, 0:TH, :]
                    nc.vector.tensor_tensor(tile, tile, alibi[:, :, P * par:P * par + 2 * P],
                                            ALU.mult).then_inc(table_ready, 1)
                if next1:
                    dve.wait_ge(lo_ready, i + 2)
                    nc.vector.tensor_copy(parts[:, 1 - par, 0:H, 2:4, :],
                                          parts[:, 1 - par, 0:H, 0:2, :]).then_inc(parts_ready, 1)
                if aside:
                    aside()
                if next2:
                    dve.wait_ge(sq_done, i + 3)
                    count(dve, newton, base - NEWTON_OPS)
                    nc.vector.tensor_reduce(ss[:], sq[:].rearrange("p (h d) -> p h d", d=HD), AX.X,
                                            ALU.add).then_inc(ss_done, 1)
                    dve.wait_ge(ss_done, i + 3)
                    rsqrt_seed(ss[:], half[:, 0:2 * H], (NORM_EPS / QK_SCALE) ** 2, ALU.max, newton)
                if prev3:
                    dve.wait_ge(aggr_done, i - 2)
                    rsqrt_seed(mv[:, 1:2], half[:, 2 * H:2 * H + 1], LN_EPS, ALU.add, ln_seed, Y_SCALE)
                    dve.wait_ge(ln_seed, i - 2)
                if rounds:
                    if next2:
                        count(dve, qkn_done, i + 2)
                    count(dve, y_done, i - 3)
                    rsqrt_guess(norm[0], norm[3], newton, base)
                if rounds:
                    rsqrt_round(0, *norm)
                if rounds:
                    rsqrt_round(1, *norm)
                if prev2:
                    dve.wait_ge(wo_done, i - 1)
                    nc.vector.tensor_tensor(resid[:, i - 2, :], resid[:, i - 2, :], ps[:, VO, D:2 * D],
                                            ALU.add).then_inc(resid_done, 1)
                if rounds:
                    rsqrt_round(2, *norm)
                if next2:
                    dve.wait_ge(newton, base + NEWTON_OPS + 1)
                    count(dve, lo_ready, i + 2)
                    nc.vector.tensor_tensor(qkn[:].rearrange("p (h d) -> p h d", d=HD),
                                            ps[:, QK, :].rearrange("p (h d) -> p h d", d=HD),
                                            rnorm[:, 0:2 * H].unsqueeze(2).to_broadcast([P, 2 * H, HD]),
                                            ALU.mult).then_inc(qkn_done, 1)
                if next1:
                    dve.wait_ge(tk_done, i + 2)
                    count(dve, s_done, (i + 1) * NC)
                    for s in range(2):
                        rows = slice(64 * s, 64 * s + 64)
                        cp = nc.vector.tensor_copy(kTz[rows, s, :, :],
                                                   tr16[rows, :].rearrange("p (m t) -> p m t", m=PAIRS))
                    cp.then_inc(k_ready, 1)
                if prev2:
                    dve.wait_ge(rel_cut, 3)
                    dve.wait_ge(resid_done, i - 1)
                    count(dve, aggr_done, i - 2)
                    nc.vector.bn_stats(stats[:], resid[:, i - 2, :]).then_inc(stats_done, 1)
                if prev3:
                    dve.wait_ge(rel_cut, 3)
                    dve.wait_ge(newton, base + NEWTON_OPS + 1)
                    nc.vector.tensor_scalar(resid[:, i - 3, :], resid[:, i - 3, :], mv[:, 0:1],
                                            rnorm[:, 2 * H:2 * H + 1], ALU.subtract, ALU.mult).then_inc(y_done, 1)
                if prev2:
                    dve.wait_ge(rel_cut, 3)
                    dve.wait_ge(stats_done, i - 1)
                    count(dve, y_done, i - 2)
                    nc.vector.bn_aggr(mv[:], stats[:]).then_inc(aggr_done, 1)

            dve.wait_ge(rel_cut, 3)
            nc.vector.tensor_copy(rel[:], rel_i[:]).then_inc(rel_f, 1)
            dve.wait_ge(rel_f, 1)
            nc.vector.tensor_scalar(far_key[:], rel[:, 0, 0:1], float(P), None, ALU.add).then_inc(rel_f, 1)
            nc.vector.memset(vsb[:], 1.0).then_inc(consts, 1)
            nc.vector.memset(ps[:, OT, :], 0.0).then_inc(consts, 1)
            nc.vector.memset(mean_ones[:], 1.0 / HID).then_inc(consts, 1)
            dve.wait_ge(alibi_done, 1)
            def abs_w2():
                dve.wait_ge(w2_in, 16)
                dve.wait_ge(sgn_ready, 1)
                nc.vector.tensor_tensor(w2_t[:], w2_t[:], sgn2[:], ALU.mult).then_inc(prep, 1)

            step(-2, 0, cur=False, pv=False, prev2=False, next1=False, prev3=False)
            dve.wait_ge(w1_in, 16)
            nc.vector.tensor_reduce(alpha1[:], w1_nat[:], AX.X, ALU.add, apply_absolute_value=True).then_inc(abs_done, 1)
            step(-1, 1, cur=False, pv=False, prev2=False, prev3=False)
            step(0, 0, pv=False, prev2=False, prev3=False, aside=abs_w2)
            step(1, 1, prev2=False, prev3=False)
            dve.wait_ge(mlp_in, 16 * 3)
            dve.wait_ge(abs_done, 1)
            nc.vector.scalar_tensor_tensor(out=bound[:], in0=bias1[:], scalar=-1.0, in1=alpha1[:], op0=ALU.mult,
                                           op1=ALU.add).then_inc(abs_done, 1)
            nc.vector.tensor_tensor(hpos[:], bias1[:], alpha1[:], ALU.add).then_inc(abs_done, 1)
            dve.wait_ge(abs_done, 3)
            nc.vector.tensor_tensor(bound[:], bound[:], hpos[:], ALU.max).then_inc(abs_done, 1)
            nc.vector.tensor_scalar(alpha1[:], alpha1[:], 1.0 / (D * Y_SCALE), None, ALU.mult).then_inc(abs_done, 1)
            nc.vector.tensor_scalar(bias2[:], bias2[:], Y_SCALE, None, ALU.mult).then_inc(abs_done, 1)
            dve.wait_ge(abs_done, 6)
            nc.vector.tensor_reduce(bound1[:], bound[:], AX.X, ALU.max).then_inc(bound_done, 1)
            step(2, 0, prev3=False)
            step(3, 1)
            with dve.Fori(0, (NB - 6) // 2) as t:
                for par in range(2):
                    step(t * 2 + 4 + par, par)
            def hidden_low(n, k, par):
                if isinstance(n, int) and n == 0:
                    dve.wait_ge(hhi_first, k + 1)
                else:
                    dve.wait_ge(hhi_done, (n - 1) * HC + k + 1)
                nc.vector.scalar_tensor_tensor(out=hid[:, par, 1, k, :], in0=gelu[:, k % 4, :], scalar=h_scale[:],
                                               in1=hid[:, par, 0, k, :], op0=ALU.mult,
                                               op1=ALU.subtract).then_inc(hlo_done, 1)

            def statistics(g, b, par):
                summed = g * GB + b + 1
                dve.wait_ge(rel_cut, 3)
                dve.wait_ge(zsum, summed)
                count(dve, zaggr, summed - 1)
                nc.vector.bn_stats(zstats[:], z[:, par, b, :]).then_inc(zstat, 1)
                dve.wait_ge(rel_cut, 3)
                dve.wait_ge(zstat, summed)
                if b == 0:
                    count(dve, z_ready, g * GB)
                nc.vector.bn_aggr(zmv[:, b, :], zstats[:]).then_inc(zaggr, 1)

            def finish_group(g, par, nxt=True):
                for b in range(GB):
                    m = g * GB + b
                    dve.wait_ge(ffn2_done, m + 1)
                    if b == 0:
                        count(dve, stored[par], (g - par) * 8)
                    nc.vector.tensor_tensor(z[:, par, b, :], ps[:, (ZBANKS if nxt else LAST_ZBANKS)[b], 0:D], alpha2[:],
                                            ALU.mult).then_inc(zscaled, 1)
                    if nxt:
                        for k in (2 * b, 2 * b + 1):
                            hidden_low(g + 1, k, 1 - par)
                    if b > 0:
                        statistics(g, b - 1, par)
                statistics(g, GB - 1, par)
                dve.wait_ge(zaggr, g * GB + GB)
                rsqrt(zmv[:, :, 1], half[:, 0:GB], nt_a[:, 0:GB], nt_b[:, 0:GB], zrstd[:], LN_EPS * Y_SCALE ** 2,
                      ALU.add, znewton, g * (NEWTON_OPS + 1))
                for b in range(GB):
                    nc.vector.tensor_scalar(z[:, par, b, :], z[:, par, b, :], zmv[:, b, 0:1], zrstd[:, b:b + 1],
                                            ALU.subtract, ALU.mult).then_inc(z_ready, 1)

            step(NB - 2, 0, next2=False)
            step(NB - 1, 1, next1=False, next2=False)
            step(NB, 0, cur=False, next1=False, next2=False)
            dve.wait_ge(bound_all, 1)
            nc.vector.tensor_scalar(bound1[:], bound1[:], 1e-30, 2.0 ** -14, ALU.max, ALU.mult).then_inc(abs_done, 1)
            dve.wait_ge(abs_done, 7)
            nc.vector.reciprocal(h_scale[:], bound1[:]).then_inc(abs_done, 1)
            dve.wait_ge(abs_done, 8)
            nc.vector.tensor_scalar(h_scale[:].bitcast(I32), h_scale[:].bitcast(I32), 0x7F800000, None,
                                    ALU.bitwise_and).then_inc(abs_done, 1)
            dve.wait_ge(abs_done, 9)
            nc.vector.tensor_scalar(h_unscale[:].bitcast(I32), h_scale[:].bitcast(I32), -1.0, float(254 << 23),
                                    ALU.mult, ALU.add).then_inc(abs_done, 1)
            dve.wait_ge(abs_done, 10)
            dve.wait_ge(alpha2_done, 1)
            nc.vector.tensor_scalar(alpha2[:], ps[:, A2, 0:D], h_unscale[:], Y_SCALE, ALU.mult, ALU.mult).then_inc(prep, 1)
            step(NB + 1, 1, cur=False, pv=False, next1=False, next2=False)
            for k in range(HC):
                dve.wait_ge(gelu_done, k + 1)
                nc.vector.tensor_scalar(hid[:, 0, 0, k, :], gelu[:, k % 4, :], h_scale[:], None,
                                        ALU.mult).then_inc(hhi_first, 1)
                hidden_low(0, k, 0)
            step(NB + 2, 0, cur=False, pv=False, prev2=False, next1=False, next2=False)
            for par in range(2):
                finish_group(par, par)
            with dve.Fori(0, (NG - 4) // 2) as t:
                for par in range(2):
                    finish_group(t * 2 + 2 + par, par)
            finish_group(NG - 2, 0)
            finish_group(NG - 1, 1, nxt=False)

        @block.gpsimd
        def _(pool):
            for a in range(3):
                nc.gpsimd.iota(rel_i[:, a, :], pattern=[[-1, P]], base=P * (a % 2),
                               channel_multiplier=1).then_inc(rel_made, 1)
            nc.gpsimd.memset(id16[:], 0.0).then_inc(id_zero, 1)
            nc.gpsimd.memset(id32[:], 0.0).then_inc(id_zero, 1)
            pool.wait_ge(rel_made, 3)
            for a in range(3):
                near = a % 2
                nc.gpsimd.affine_select(out=rel_i[:, a, :], in_=rel_i[:, a, :], compare_op=ALU.is_ge, fill=FAR,
                                        base=-near, pattern=[[1 if near else -1, P]],
                                        channel_multiplier=-1 if near else 1).then_inc(rel_cut, 1)
            pool.wait_ge(id_zero, 2)
            for m in (id16, id32):
                nc.gpsimd.affine_select(out=m[:], in_=m[:], compare_op=ALU.not_equal, fill=1.0, base=0,
                                        pattern=[[-1, P]], channel_multiplier=1).then_inc(consts, 1)
            nc.gpsimd.memset(qT[:], 0.0).then_inc(consts, 1)
            nc.gpsimd.memset(kTz[:], 0.0).then_inc(consts, 1)

            def low_part(n, par):
                pool.wait_ge(hi_ready, n + 1)
                src = qkn[:].rearrange("p (h d) -> p h d", d=HD)
                nc.gpsimd.tensor_tensor(parts[:, par, 0:H, 1, :], src[:, 0:H, :], parts[:, par, 0:H, 0, :],
                                        ALU.subtract)
                nc.gpsimd.tensor_tensor(parts[:, par, H:2 * H, 2:4, :],
                                        src[:, H:2 * H, :].unsqueeze(2).to_broadcast([P, H, 2, HD]),
                                        parts[:, par, H:2 * H, 0:2, :], ALU.subtract).then_inc(lo_ready, 1)

            def cut_chunk(i, c, par):
                chunks = pool.to_reg(i * NC + c + 1)
                pool.wait_ge(alibi_done, 1)
                pool.wait_ge(exp_done, chunks)
                for near, tile in enumerate((par, 1 - par)):
                    at = prob[:, par, CH * c:CH * c + CH, P * tile:P * tile + P]
                    sel = nc.gpsimd.affine_select(out=at, in_=at, compare_op=ALU.is_ge, fill=0.0, base=-near,
                                                  pattern=[[0, CH], [1 if near else -1, P]],
                                                  channel_multiplier=-1 if near else 1)
                sel.then_inc(cut_ready, 1)

            def step(i, par, next2=True):
                for c in range(1, NC):
                    cut_chunk(i, c, par)
                if next2:
                    low_part(i + 2, par)

            low_part(0, 0)
            low_part(1, 1)
            with pool.Fori(0, (NB - 2) // 2) as t:
                for par in range(2):
                    step(t * 2 + par, par)
            step(NB - 2, 0, next2=False)
            step(NB - 1, 1, next2=False)

            pool.wait_ge(bound_done, 1)
            nc.gpsimd.partition_all_reduce(bound1[:], bound1[:], P, bass.bass_isa.ReduceOp.max).then_inc(bound_all, 1)

            def low_y(n, b):
                m = n * GB + b
                blocks = m + 1
                pool.wait_ge(alibi_done, 1)
                pool.wait_ge(yhi_done, blocks)
                nc.gpsimd.tensor_tensor(yparts[:, b, 1, :], resid[:, m, :], yparts[:, b, 0, :],
                                        ALU.subtract).then_inc(ylo_done, 1)

            def add_b2(n, b):
                m = n * GB + b
                blocks = m + 1
                pool.wait_ge(alibi_done, 1)
                pool.wait_ge(ylo_done, blocks)
                nc.gpsimd.tensor_tensor(resid[:, m, :], resid[:, m, :], bias2[:], ALU.add).then_inc(yb_done, 1)

            def add_residual(g, b, par):
                m = g * GB + b
                blocks = m + 1
                pool.wait_ge(alibi_done, 1)
                pool.wait_ge(yb_done, blocks)
                pool.wait_ge(zscaled, blocks)
                nc.gpsimd.tensor_tensor(z[:, par, b, :], z[:, par, b, :], resid[:, m, :], ALU.add).then_inc(zsum, 1)

            def group_step(g, par, nxt2=True):
                if nxt2:
                    low_y(g + 2, 0)
                    low_y(g + 2, 1)
                    add_b2(g + 2, 0)
                    add_b2(g + 2, 1)
                add_residual(g, 0, par)
                if nxt2:
                    low_y(g + 2, 2)
                    low_y(g + 2, 3)
                for b in range(1, GB):
                    add_residual(g, b, par)
                    if nxt2 and b < GB - 1:
                        add_b2(g + 2, b + 1)

            for n in range(2):
                for b in range(GB):
                    low_y(n, b)
                    if n == 0:
                        add_b2(n, b)
            for b in range(GB):
                add_b2(1, b)
            with pool.Fori(0, (NG - 2) // 2) as t:
                for par in range(2):
                    group_step(t * 2 + par, par)
            group_step(NG - 2, 0, nxt2=False)
            group_step(NG - 1, 1, nxt2=False)


_OUT = "out_dram"


def kernel(L0_attn_x, L0_attn_Wq, L0_attn_Wk, L0_attn_Wv, L0_attn_Wo, L0_ffn_w1, L0_ffn_b1, L0_ffn_w2, L0_ffn_b2):
    import concourse.bacc as bacc
    from concourse.bass_utils import run_bass_kernel_spmd

    def cont(a):
        return np.ascontiguousarray(a)

    x = np.asarray(L0_attn_x).reshape(NB, P, D)
    wqkv = np.concatenate([np.asarray(w) for w in (L0_attn_Wq, L0_attn_Wk, L0_attn_Wv)], axis=0)
    arrays = {
        "x": cont(x),
        "xT": cont(x.reshape(NB, P, DC, P).transpose(0, 3, 2, 1)),
        "wqkvT": cont(wqkv.T.reshape(DC, P, 3 * D).transpose(1, 0, 2)),
        "woT": cont(np.asarray(L0_attn_Wo).T.reshape(DC, P, D).transpose(1, 0, 2)),
        "w1": cont(np.asarray(L0_ffn_w1).reshape(HC, P, D).transpose(1, 0, 2)),
        "w1T": cont(np.asarray(L0_ffn_w1).T.reshape(DC, P, HID).transpose(1, 0, 2)),
        "b1c": cont(np.asarray(L0_ffn_b1).reshape(HC, P).T),
        "w2T": cont(np.asarray(L0_ffn_w2).T.reshape(HC, P, D).transpose(1, 0, 2)),
        "b2": cont(np.broadcast_to(np.asarray(L0_ffn_b2), (P, D))),
    }
    nc = bacc.Bacc("TRN2", target_bir_lowering=False, num_devices=1)
    args = [nc.dram_tensor(f"in_{n}", a.shape, F32, kind="ExternalInput").ap() for n, a in arrays.items()]
    out = nc.dram_tensor(_OUT, (T, D), F32, kind="ExternalOutput").ap()
    build(nc, *args, out.rearrange("(g b p) d -> g p b d", b=GB, p=P))
    r = run_bass_kernel_spmd(nc, [{f"in_{n}": a for n, a in arrays.items()}], core_ids=[0])
    return r.results[0][_OUT].reshape(1, T, D)
```
